# Optimizing a Trainium2 kernel written in Bass

```python
import numpy as np
import jax
import jax.numpy as jnp

def _softmax(x, axis=-1):
    return jax.nn.softmax(x, axis=axis)

def _gelu(x):
    return jax.nn.gelu(x, approximate=True)

def _silu(x):
    return jax.nn.silu(x)

def _sigmoid(x):
    return jax.nn.sigmoid(x)

def _layernorm(x, axis=-1, eps=1e-05):
    m = jnp.mean(x, axis=axis, keepdims=True)
    v = jnp.var(x, axis=axis, keepdims=True)
    return (x - m) / jnp.sqrt(v + eps)

def _scatter_add(tgt, idx, src, axis=0):
    return tgt.at[idx].add(src)

def _segment_sum(src, seg, n):
    return jax.ops.segment_sum(src, seg, n)
kernel_name = 'mk_prb_d1_jaxref_r8_c9dc63'

def setup_inputs(seed: int=0):
    np.random.seed(seed)
    _w = jnp.asarray

    def _L0_attn_setup():
        import jax, jax.numpy as jnp
        import numpy as np
        HEADS = 16
        SCALE = 8.0
        EPS = 1e-12

        def _l2norm(t):
            n = jnp.sqrt(jnp.sum(t * t, axis=-1, keepdims=True))
            return t / jnp.maximum(n, EPS)
        key = jax.random.key(seed)
        k0, k1, k2, k3, k4 = jax.random.split(key, 5)
        b, n, d = (1, 512, 128)
        w_scale = 1.0 / np.sqrt(d)
        return {'x': jax.random.normal(k0, (b, n, d), dtype=jnp.float32), 'Wq': jax.random.normal(k1, (d, d), dtype=jnp.float32) * w_scale, 'Wk': jax.random.normal(k2, (d, d), dtype=jnp.float32) * w_scale, 'Wv': jax.random.normal(k3, (d, d), dtype=jnp.float32) * w_scale, 'Wo': jax.random.normal(k4, (d, d), dtype=jnp.float32) * w_scale}
    _L0_attn_in = _L0_attn_setup()

    def _L0_ffn_setup():
        import jax, jax.numpy as jnp
        import numpy as np
        B, S, H, M, E, K = (4, 256, 128, 512, 8, 2)
        key = jax.random.key(seed)
        ks = jax.random.split(key, 6)
        x = jax.random.normal(ks[0], (B, S, H), dtype=jnp.float32)
        Wr = jax.random.normal(ks[1], (E, H), dtype=jnp.float32) * (1.0 / np.sqrt(H))
        W1 = jax.random.normal(ks[2], (E, M, H), dtype=jnp.float32) * np.sqrt(2.0 / (H + M))
        b1 = jax.random.normal(ks[3], (E, M), dtype=jnp.float32) * 1e-06
        W2 = jax.random.normal(ks[4], (E, H, M), dtype=jnp.float32) * np.sqrt(2.0 / (H + M))
        b2 = jax.random.normal(ks[5], (E, H), dtype=jnp.float32) * 1e-06
        return {'x': x, 'Wr': Wr, 'W1': W1, 'b1': b1, 'W2': W2, 'b2': b2}
    _L0_ffn_in = _L0_ffn_setup()
    _d = {'L0_attn_x': _L0_attn_in['x'], 'L0_attn_Wq': _L0_attn_in['Wq'], 'L0_attn_Wk': _L0_attn_in['Wk'], 'L0_attn_Wv': _L0_attn_in['Wv'], 'L0_attn_Wo': _L0_attn_in['Wo'], 'L0_ffn_Wr': _L0_ffn_in['Wr'], 'L0_ffn_W1': _L0_ffn_in['W1'], 'L0_ffn_b1': _L0_ffn_in['b1'], 'L0_ffn_W2': _L0_ffn_in['W2'], 'L0_ffn_b2': _L0_ffn_in['b2']}
    _x0 = _d['L0_attn_x']
    _d['L0_attn_x'] = jax.random.normal(jax.random.fold_in(jax.random.key(seed), 1), (16, 512, 128), dtype=_x0.dtype)
    del _x0
    return _d

def reference(L0_attn_x, L0_attn_Wq, L0_attn_Wk, L0_attn_Wv, L0_attn_Wo, L0_ffn_Wr, L0_ffn_W1, L0_ffn_b1, L0_ffn_W2, L0_ffn_b2):

    def _L0_attn_ref(x, Wq, Wk, Wv, Wo):
        import jax, jax.numpy as jnp
        import numpy as np
        HEADS = 16
        SCALE = 8.0
        EPS = 1e-12

        def _l2norm(t):
            n = jnp.sqrt(jnp.sum(t * t, axis=-1, keepdims=True))
            return t / jnp.maximum(n, EPS)
        b, n, d = x.shape
        h = HEADS
        dh = d // h

        def proj(W):
            y = jnp.einsum('bnd,df->bnf', x, W)
            return y.reshape(b, n, h, dh).transpose(0, 2, 1, 3)
        q, k, v = (proj(Wq), proj(Wk), proj(Wv))
        q = _l2norm(q)
        k = _l2norm(k)
        sim = jnp.einsum('bhid,bhjd->bhij', q, k) * SCALE
        mask_value = -jnp.finfo(sim.dtype).max
        causal = jnp.triu(jnp.ones((n, n), dtype=bool), 1)
        sim = jnp.where(causal, mask_value, sim)
        attn = jax.nn.softmax(sim, axis=-1)
        o = jnp.einsum('bhij,bhjd->bhid', attn, v)
        o = o.transpose(0, 2, 1, 3).reshape(b, n, d)
        return jnp.einsum('bnf,fd->bnd', o, Wo)

    def _L0_ffn_ref(x, Wr, W1, b1, W2, b2):
        import jax, jax.numpy as jnp
        import numpy as np
        B, S, H, M, E, K = (4, 256, 128, 512, 8, 2)
        logits = jnp.einsum('bsh,eh->bse', x, Wr)
        probs = jax.nn.softmax(logits, axis=-1)
        top_v, top_i = jax.lax.top_k(probs, K)
        top_v = top_v / jnp.sum(top_v, axis=-1, keepdims=True)
        out = jnp.zeros_like(x)
        for e in range(E):
            w_e = jnp.sum(jnp.where(top_i == e, top_v, 0.0), axis=-1)
            h = jnp.einsum('bsh,mh->bsm', x, W1[e]) + b1[e]
            h = jax.nn.gelu(h, approximate=False)
            y = jnp.einsum('bsm,hm->bsh', h, W2[e]) + b2[e]
            out = out + y * w_e[..., None]
        return out
    x = L0_attn_x
    xn = _layernorm(x, axis=-1)
    x = x + _L0_attn_ref(xn, L0_attn_Wq, L0_attn_Wk, L0_attn_Wv, L0_attn_Wo) + _L0_ffn_ref(xn, L0_ffn_Wr, L0_ffn_W1, L0_ffn_b1, L0_ffn_W2, L0_ffn_b2)
    return x

_drawn_inputs = setup_inputs


def setup_inputs(seed=0):
    import zlib

    import numpy as np

    out = dict(_drawn_inputs(seed))
    spreads = {}
    factors = {}
    for name, (base, spread) in spreads.items():
        noise = np.random.default_rng([zlib.crc32(name.encode()), seed]).standard_normal(out[name].shape)
        drawn = base * np.exp(spread * noise) if base else spread * noise
        out[name] = jnp.asarray(drawn.astype(out[name].dtype))
    for name, factor in factors.items():
        out[name] = (out[name] * factor).astype(out[name].dtype)
    return out
```

```python
from contextlib import ExitStack

import concourse.bass as bass
from concourse import mybir

P = 128
ALU = mybir.AluOpType
ACT = mybir.ActivationFunctionType
AX = mybir.AxisListType
F32 = mybir.dt.float32
F16 = mybir.dt.float16
I32 = mybir.dt.int32


def build(nc, x, Wq, Wk, Wv, Wo, Wr, W1, b1, W2_, b2, out):
    NB, N, D = x.shape
    E, M, _ = W1.shape
    H, DH = 16, D // 16
    TB = N // P
    T = NB * TB
    QH, NQ = 4, H // 4
    MC = M // P
    TOPK = 2
    FJ = 2
    FT = FJ * P
    FSH = FT.bit_length() - 1
    FFN_TILES = (TOPK * NB * N + E * (FT - 1)) // FT
    SLOTS = FFN_TILES * FT
    HALF = NB // 2
    SCALE, NORM_EPS, LN_EPS = 8.0, 1e-12, 1e-5
    UP = 64.0
    NQK = 2 * H
    WV0, WEND = E + 2 * D, E + 3 * D
    B1C, W2C, B2C = M, M + MC, 2 * M + MC
    WX = B2C + D
    UN = 5
    UW = 1024
    PARTS = [(0, 0, P, N - P), (0, N - P, 0, P), (3, N, 3 * P, P), (1, N + P, P, N - P)]
    DIAG = N - P

    with ExitStack() as ctx:
        def sb(name, shape, dt=F32):
            return ctx.enter_context(nc.sbuf_tensor(name, shape, dt))

        def sem(name):
            return ctx.enter_context(nc.semaphore(name))

        def sems(names):
            return [sem(n) for n in names.split()]

        def pair(name):
            return [sem(f"{name}{s}") for s in range(2)]

        def dram(name, shape, dt=F32):
            return nc.dram_tensor(name, shape, dt).ap()

        xn_rows = dram("xn_rows", [NB, N, D])
        xn_cols = dram("xn_cols", [NB, D, N])
        slot_x = dram("slot_x", [SLOTS + FJ * E * P, D])
        slot_y = dram("slot_y", [SLOTS, D])

        identf = sb("identf", [P, P])
        identh = sb("identh", [P, P], F16)
        before = sb("before", [P, P])
        ones = sb("ones", [P, P])
        causal = sb("causal", [P, P])
        zeros = sb("zeros", [P, D])
        back = sb("back", [P, E])
        starts = sb("starts", [P, FFN_TILES])
        consti = sb("consti", [P, E + FFN_TILES], I32)
        wall = sb("wall", [P, WEND])
        wo = sb("wo", [P, D])
        wexp = sb("wexp", [P, E, WX])
        b1n = sb("b1n", [E * MC, P])

        acc = sb("acc", [P, T, D])

        xs = sb("xs", [P, 2, TB, D])
        bst = sb("bst", [P, 2, TB, 6])
        mv = sb("mv", [P, 2, TB, 2])
        std = sb("std", [P, 2, TB])
        rstd = sb("rstd", [P, 2, TB])
        xns = sb("xns", [P, 2, TB, D])
        xts = sb("xts", [P, 2, N])
        logits = sb("logits", [P, T, E])
        norms = sb("norms", [P, T, NQK])

        prob = sb("prob", [P, 2, UN, UW])
        flat_prob = prob[:].rearrange("p a u w -> p (a u w)")
        w1n = flat_prob[:, 0:M].rearrange("p (c d) -> p c d", c=MC)
        w2n = flat_prob[:, M:2 * M]
        sq = flat_prob[:, 2 * M:2 * M + 2 * TB * 2 * D].rearrange("p (s t c) -> p s t c", s=2, t=TB)

        hot = sb("hot", [P, TOPK, T, E])
        both = sb("both", [P, T, E])
        top = sb("top", [P, TOPK, T])
        rk = sb("rk", [P, TOPK, T])
        cnt = sb("cnt", [P, 5, 2 * E])
        cnti = sb("cnti", [P, 2, E], I32)
        slotf = sb("slotf", [P, TOPK, T])
        slots = sb("slots", [P, T, TOPK], I32)
        gate = sb("gate", [P, TOPK, T])
        tile_f = sb("tile_f", [P, 2, FFN_TILES])
        tile_i = sb("tile_i", [P, FFN_TILES], I32)
        padi = sb("padi", [P, 2, FJ * E], I32)
        padf = sb("padf", [P, 5, FJ * E])
        pads = sb("pads", [P, FJ * E], I32)

        xt = sb("xt", [P, N])
        rnb = sb("rnb", [P, TB, NQK])
        qn = sb("qn", [P, NQK, DH])
        dup = sb("dup", [P, TB, 2, H, 4 * DH], F16)
        qks = sb("qks", [P, NQ, 2, N], F16)
        ks = sb("ks", [P, QH, NQ, N], F16)
        vn = sb("vn", [P, TB * H, DH])
        v = sb("v", [P, TB * H, DH + 1])
        rs = sb("rs", [P, TB, QH])
        turn = sb("turn", [P, 3 * N])
        osb = turn[:, 0:N]
        on = turn[:, N:2 * N].rearrange("p (t d) -> p t d", t=TB)
        ot = turn[:, 2 * N:3 * N]
        pre = turn[:, 0:3 * T * E].rearrange("p (s t e) -> p s t e", s=2, e=E)

        idx = sb("idx", [P, 2, TB, TOPK], I32)
        rows = sb("rows", [P, 2, TOPK, TB, D])
        lg2 = rows[:, 0, 1].rearrange("p t (u e) -> p (t u) e", e=E)
        tmp = rows[:, 1, 1].rearrange("p t (u e) -> p (t u) e", e=E)
        flat_rows = rows[:].rearrange("p a c t d -> p (a c t d)")
        xg = flat_rows[:, 0:2 * FT].rearrange("p (s j d) -> p s j d", s=2, j=FJ)
        xgt = flat_rows[:, 2 * FT:4 * FT].rearrange("p (s n) -> p s n", s=2)
        ys = flat_rows[:, 4 * FT:6 * FT].rearrange("p (s j d) -> p s j d", s=2, j=FJ)
        hs = flat_prob[:, 0:2 * MC * FT].rearrange("p (s c n) -> p s c n", s=2, c=MC)
        ws = flat_prob[:, 2 * MC * FT:2 * MC * FT + 2 * WX].rearrange("p (s w) -> p s w", s=2)
        assert 2 * MC * FT + 2 * WX <= UN * UW and D == P and NB * TB * E == 512

        psum = ctx.enter_context(nc.psum_tensor("psum", [P, 8, 512], F32))
        score = [psum[:, 2 * s:2 * s + 2, :].rearrange("p a b -> p (a b)") for s in range(2)]
        ps_o, ps_pa, ps_pc = psum[:, 4, :], psum[:, 5, :], psum[:, 7, :]
        ps_pb = psum[:, 6, :].bitcast(F16)

        made, zero_made, pad_made = sems("made zero_made pad_made")
        w_in, wv_in, acc_in, b1_in, b2_in, wn_in = sems("w_in wv_in acc_in b1_in b2_in wn_in")
        xs_in, rows_out, cols_out = pair("xs_in"), pair("rows_out"), pair("cols_out")
        stats, mv_ready, std_ready, rstd_ready, xn_ready = sems("stats mv_ready std_ready rstd_ready xn_ready")
        tr_done, xts_ready, joint_done, sq_ready, ss_ready = sems("tr_done xts_ready joint_done sq_ready ss_ready")
        floored, norms_ready, zeroed, padded = sems("floored norms_ready zeroed padded")
        wtr_done, wt_ready, btr_done, bt_ready = sems("wtr_done wt_ready btr_done bt_ready")
        r_step, chosen, counted, totals_read, routed = sems("r_step chosen counted totals_read routed")
        gap_ready, gap_exp, gates_ready = sems("gap_ready gap_exp gates_ready")
        xt_in, proj_done, rn_done, qn_done, proj_evac = sems("xt_in proj_done rn_done qn_done proj_evac")
        hi_done, dup_done, qktr_done, qk_evac = sems("hi_done dup_done qktr_done qk_evac")
        ks_in = [sem(f"ks_in{q}") for q in range(NQ)]
        scored, exp_done, masked, masked2 = sems("scored exp_done masked masked2")
        v_ready, pv_done, o_evac, otr_done = sems("v_ready pv_done o_evac otr_done")
        rs_done, norm_done, ontr_done, ot_ready = sems("rs_done norm_done ontr_done ot_ready")
        outp_done, added, idx_ready, combined, stored = sems("outp_done added idx_ready combined stored")
        rows_in, moved, xg_in, y_out = pair("rows_in"), pair("moved"), pair("xg_in"), pair("y_out")
        xgtr_done, xgt_ready, w1_ready, w2_ready, hid_done = sems("xgtr_done xgt_ready w1_ready w2_ready hid_done")
        gelu_done, y_done, ys_ready = sems("gelu_done y_done ys_ready")

        block = ctx.enter_context(nc.Block())

        def some(count):
            return not isinstance(count, int) or count > 0

        def counted_by(eng, count):
            return count if isinstance(count, int) else eng.to_reg(count)

        def known(i, value):
            return isinstance(i, int) and i == value

        def at(i, n=1):
            return slice(i, i + n) if isinstance(i, int) else bass.ds(i, n)

        def batch_rows(t, b):
            return t.rearrange("b (t p) d -> p (b t) d", p=P)[:, at(TB * b, TB), :]

        def batch_cols(b):
            return xn_cols.rearrange("b d n -> d b n")[:, at(b), :].rearrange("d b n -> d (b n)")

        def tile_rows(t, k):
            return t.rearrange("(u p) d -> p u d", p=P)[:, at(FJ * k, FJ), :]

        def stage_a(eng, step):
            step(0)
            step(1)
            with eng.Fori(2, NB // 2) as i:
                step(i)

        def attention(eng, body, between):
            body(0)
            body(1)
            with eng.Fori(2, HALF) as b:
                body(b)
            between()
            body(HALF, second=True)
            with eng.Fori(HALF + 1, NB - 1) as b:
                body(b, second=True)
            body(NB - 1, second=True, last=True)

        def expert_tiles(eng, step):
            for k in range(4):
                step(k, k % 2)
            with eng.Fori(2, FFN_TILES // 2 - 1) as i:
                step(2 * i, 0)
                step(2 * i + 1, 1)
            for k in range(2 * (FFN_TILES // 2 - 1), FFN_TILES):
                step(k, k % 2)

        @block.sync
        def _(sp):
            sp.dma_start(wall[:, 0:E], Wr.rearrange("e d -> d e"), allow_slow_non_contiguous=True).then_inc(w_in, 16)
            sp.dma_start(wall[:, E:E + D], Wq).then_inc(w_in, 16)
            sp.dma_start(wall[:, E + D:WV0], Wk).then_inc(w_in, 16)

            def load(i):
                for s in range(2):
                    if some(2 * i + s - 1):
                        sp.wait_ge(xn_ready, 2 * i + s - 1)
                    sp.dma_start(xs[:, s], batch_rows(x, 2 * i + s)).then_inc(xs_in[s], 16)
                if some(2 * i):
                    sp.wait_ge(wtr_done, 2 * i)
                w1_e = W1.rearrange("e (c m) d -> m (e c) d", m=P)[:, at(MC * i, MC), :]
                sp.dma_start(w1n, w1_e).then_inc(wn_in, 16)
                w2_e = W2_.rearrange("e d m -> d e m")[:, at(i), :].rearrange("d e m -> d (e m)")
                sp.dma_start(w2n, w2_e).then_inc(wn_in, 16)

            def store(i):
                for s in range(2):
                    sp.wait_ge(xn_ready, 2 * i + s + 1)
                    sp.dma_start(batch_rows(xn_rows, 2 * i + s), xns[:, s]).then_inc(rows_out[s], 16)
                for s in range(2):
                    sp.wait_ge(xts_ready, 2 * i + s + 1)
                    sp.dma_start(batch_cols(2 * i + s), xts[:, s]).then_inc(cols_out[s], 16)

            def step(i):
                load(i)
                if not known(i, 0):
                    store(i - 1)
            stage_a(sp, step)
            store(NB // 2 - 1)
            sp.dma_start(wall[:, WV0:WEND], Wv).then_inc(wv_in, 16)
            sp.dma_start(wo[:], Wo).then_inc(wv_in, 16)
            sp.dma_start(b1n[:], b1.rearrange("e (c m) -> (e c) m", m=P)).then_inc(b1_in, 16)
            b2_all = b2.rearrange("e d -> (e d)").rearrange("(a e d) -> a e d", a=1, e=E).broadcast_to([P, E, D])
            sp.dma_start(wexp[:, :, B2C:WX], b2_all).then_inc(b2_in, 16)

            def load_xt(b):
                if some(TB * b):
                    sp.wait_ge(proj_done, TB * b)
                sp.dma_start(xt[:], batch_cols(b)).then_inc(xt_in, 16)

            def spread_k(m, q):
                sp.wait_ge(qk_evac, m + 1)
                for g in range(QH):
                    r = slice(32 * g, 32 * g + 32)
                    sp.dma_start(ks[r, g, q, :], qks[r, q, 1, :]).then_inc(ks_in[q], 16)

            for s in range(2):
                sp.wait_ge(cols_out[s], 16 * (NB // 2))
                sp.wait_ge(rows_out[s], 16 * (NB // 2))
            load_xt(0)
            sp.wait_ge(made, 4)
            spread_k(0, 0)
            spread_k(1, 1)
            sp.wait_ge(zero_made, 1)
            spare = slot_x.rearrange("(u p) d -> p u d", p=P)[:, TOPK * T:SLOTS // P, :]
            nothing = zeros[:].rearrange("p (a d) -> p a d", a=1).broadcast_to([P, SLOTS // P - TOPK * T, D])
            sp.dma_start(spare, nothing).then_inc(zeroed, 16)

            def load_acc(half):
                acc_rows = x.rearrange("b (t p) d -> p (b t) d", p=P)
                tiles = slice(half * T // 2, (half + 1) * T // 2)
                sp.dma_start(acc[:, tiles, :], acc_rows[:, tiles, :]).then_inc(acc_in, 16)
            load_acc(0)

            def load_rows(b, j):
                if some(16 * TB * TOPK * b):
                    sp.wait_ge(moved[j], 16 * TB * TOPK * b)
                sp.dma_start(rows[:, j, 0], batch_rows(xn_rows, 2 * b + j)).then_inc(rows_in[j], 16)

            def body(b, second=False, last=False):
                n = NQ * b
                if not last:
                    load_xt(b + 1)
                if not second:
                    if isinstance(b, int):
                        sp.wait_ge(routed, 1)
                    load_rows(b, 0)
                spread_k(n + 2, 2)
                spread_k(n + 3, 3)
                if not second:
                    load_rows(b, 1)
                if second and not known(b, HALF):
                    count = counted_by(sp, 2 * TB * TOPK * (b - HALF))
                    sp.wait_ge(made, 1)
                    sp.wait_ge(combined, count)
                    sp.wait_ge(added, b - 1)
                    k = 2 * (b - HALF - 1)
                    sp.dma_start(batch_rows(out, k), acc[:, at(TB * k, TB), :]).then_inc(stored, 16)
                    sp.dma_start(batch_rows(out, k + 1), acc[:, at(TB * (k + 1), TB), :]).then_inc(stored, 16)
                if not last:
                    spread_k(n + NQ, 0)
                    spread_k(n + NQ + 1, 1)

            def load_tile(k, s):
                if some(k - 1):
                    sp.wait_ge(xgtr_done, k - 1)
                sp.dma_start(xg[:, s], tile_rows(slot_x, k)).then_inc(xg_in[s], 16)

            def store_tile(k, s):
                sp.wait_ge(ys_ready, k + 1)
                sp.dma_start(tile_rows(slot_y, k), ys[:, s]).then_inc(y_out[s], 16)

            def between():
                load_acc(1)
                for j in range(2):
                    sp.wait_ge(moved[j], 16 * TB * TOPK * HALF)
                sp.wait_ge(padded, 16 * FJ * E)
                for k in range(3):
                    load_tile(k, k % 2)

                def step(k, s):
                    if not isinstance(k, int) or k + 3 < FFN_TILES:
                        load_tile(k + 3, 1 - s)
                    if not known(k, 0):
                        store_tile(k - 1, 1 - s)
                expert_tiles(sp, step)
                store_tile(FFN_TILES - 1, (FFN_TILES - 1) % 2)

            attention(sp, body, between)
            sp.wait_ge(combined, 2 * TB * TOPK * (NB - HALF))
            sp.wait_ge(added, NB)
            for k in (NB - 2, NB - 1):
                sp.dma_start(batch_rows(out, k), acc[:, at(TB * k, TB), :]).then_inc(stored, 16)
            sp.wait_ge(stored, 16 * NB)

        @block.gpsimd
        def _(pool):
            pool.memset(zeros[:], 0.0).then_inc(zero_made, 1)
            pool.memset(identf[:], 1.0)
            pool.memset(identh[:], 1.0)
            pool.memset(before[:], 1.0)
            pool.memset(causal[:], 1.0)
            pool.iota(consti[:, 0:E], pattern=[[-1, E]], base=E, channel_multiplier=0)
            pool.iota(consti[:, E:], pattern=[[FT, FFN_TILES]], base=0, channel_multiplier=0)
            pool.memset(ones[:], 1.0).then_inc(made, 1)
            pool.wait_ge(made, 1)
            for m in (identf, identh):
                pool.affine_select(out=m[:], in_=m[:], compare_op=ALU.is_equal, fill=0.0, base=0,
                                   pattern=[[-1, P]], channel_multiplier=1)
            pool.affine_select(out=before[:], in_=before[:], compare_op=ALU.is_gt, fill=0.0, base=0,
                               pattern=[[1, P]], channel_multiplier=-1)
            pool.affine_select(out=causal[:], in_=causal[:], compare_op=ALU.is_ge, fill=0.0, base=0,
                               pattern=[[1, P]], channel_multiplier=-1).then_inc(made, 1)
            pool.iota(padi[:, 0], pattern=[[P, FJ], [0, E]], base=0, channel_multiplier=1)
            pool.iota(padi[:, 1], pattern=[[P, FJ * E]], base=SLOTS, channel_multiplier=1).then_inc(pad_made, 1)
            pool.wait_ge(pad_made, 1)
            pool.tensor_copy(padf[:, 0], padi[:, 0])
            pool.tensor_copy(padf[:, 4], padi[:, 1])
            pool.tensor_copy(back[:], consti[:, 0:E])
            pool.tensor_copy(starts[:], consti[:, E:])
            pool.memset(v[:], 1.0)
            pool.memset(cnt[:], 0.0).then_inc(made, 1)
            pool.memset(ks[:], 0.0).then_inc(made, 1)

            def move(b, j, t, second):
                if t == 0:
                    if some(16 * TB * TOPK * b):
                        pool.wait_ge(moved[j], 16 * TB * TOPK * b)
                    k = 2 * (b - HALF) + j if second else 2 * b + j
                    pool.tensor_copy(idx[:, j], slots[:, at(TB * k, TB), :]).then_inc(idx_ready, 1)
                    count = counted_by(pool, 2 * b + j + 1)
                    pool.wait_ge(made, 1)
                    pool.wait_ge(idx_ready, count)
                    if second:
                        count = counted_by(pool, 2 * TB * TOPK * (b - HALF) + (j - 1) * TB * TOPK)
                        pool.wait_ge(made, 1)
                        if some(count):
                            pool.wait_ge(combined, count)
                    else:
                        count = counted_by(pool, 16 * (b + 1))
                        pool.wait_ge(made, 1)
                        pool.wait_ge(rows_in[j], count)
                for c in range(TOPK):
                    where = bass.IndirectOffsetOnAxis(ap=idx[:, j, t, c:c + 1], axis=0)
                    if second:
                        pool.indirect_dma_start(rows[:, j, c, t, :], None, slot_y, where).then_inc(moved[j], 16)
                    else:
                        pool.indirect_dma_start(slot_x, where, rows[:, j, 0, t, :], None).then_inc(moved[j], 16)

            def body(b, second=False, last=False):
                if known(b, 0):
                    pool.wait_ge(routed, 1)
                    pool.wait_ge(zeroed, 16)
                if not second and isinstance(b, int):
                    for c in range(FJ * E // 2):
                        c += b * (FJ * E // 2)
                        where = bass.IndirectOffsetOnAxis(ap=pads[:, c:c + 1], axis=0)
                        pool.indirect_dma_start(slot_x, where, zeros[:], None).then_inc(padded, 16)
                if known(b, HALF):
                    for s in range(2):
                        pool.wait_ge(y_out[s], 16 * ((FFN_TILES + 1 - s) // 2))
                for q in range(NQ):
                    n = NQ * b + q
                    for g in range(1, QH, 2):
                        count = counted_by(pool, UN * n + g + 1)
                        pool.wait_ge(made, 1)
                        pool.wait_ge(exp_done, count)
                        p = prob[:, q % 2, g - 1:g + 1, DIAG:DIAG + 3 * P].rearrange("p g (a c) -> p g a c", a=3)
                        pool.affine_select(out=p, in_=p, compare_op=ALU.is_ge, fill=0.0, base=0,
                                           pattern=[[0, 2], [0, 3], [1, P]], channel_multiplier=-1).then_inc(masked, 1)
                        move(b, q // 2, 2 * (q % 2) + g // 2, second)
            attention(pool, body, lambda: None)

        @block.scalar
        def _(act):
            def deviation(i):
                for s in range(2):
                    act.wait_ge(mv_ready, 2 * i + s + 1)
                    act.activation(std[:, s], mv[:, s, :, 1], ACT.Sqrt).then_inc(std_ready, 1)

            def squares(i):
                for s in range(2):
                    for t in range(TB):
                        tile = TB * (2 * i + s) + t
                        if t == 0:
                            if some(2 * i + s - 1):
                                act.wait_ge(ss_ready, 2 * i + s - 1)
                        act.wait_ge(joint_done, tile + 1)
                        act.activation(sq[:, s, t, :], psum[:, 2 + t, E:WV0], ACT.Square)
                        act.copy(logits[:, at(tile), :], psum[:, 2 + t, 0:E].rearrange("p (a e) -> p a e", a=1))\
                            .then_inc(sq_ready, 1)

            def step(i):
                deviation(i)
                if not known(i, 0):
                    squares(i - 1)
                for s in range(2):
                    act.wait_ge(tr_done, 2 * i + s + 1)
                    if some(16 * i):
                        act.wait_ge(cols_out[s], 16 * i)
                    act.copy(xts[:, s], psum[:, s, :]).then_inc(xts_ready, 1)
                for k in range(2):
                    act.wait_ge(wtr_done, 2 * i + k + 1)
                    w = wexp[:, at(i), k * W2C:k * W2C + M]
                    act.copy(w, psum[:, 6 + k, :].rearrange("p (a m) -> p a m", a=1)).then_inc(wt_ready, 1)
            stage_a(act, step)
            squares(NB // 2 - 1)
            act.wait_ge(floored, 1)
            act.activation(norms[:], norms[:], ACT.Sqrt, scale=1.0 / UP ** 2).then_inc(norms_ready, 1)

            def body(b, second=False, last=False):
                for q in range(NQ):
                    n = NQ * b + q
                    for u in range(UN):
                        act.wait_ge(scored, UN * n + u + 1)
                        if u == 0:
                            if some(n - 1):
                                act.wait_ge(pv_done, n - 1)
                        act.activation(prob[:, q % 2, u, :], score[(q + u) % 2], ACT.Exp,
                                       scale=SCALE / UP ** 2).then_inc(exp_done, 1)

            def gelus(k, s):
                for c in range(MC):
                    if c % 2 == 0:
                        act.wait_ge(hid_done, 2 * k + c // 2 + 1)
                    if c == 0:
                        if some(k - 1):
                            act.wait_ge(y_done, k - 1)
                    act.activation(hs[:, s, c, :], psum[:, 2 * s + c // 2, (c % 2) * FT:(c % 2 + 1) * FT],
                                   ACT.Gelu, bias=ws[:, s, B1C + c:B1C + c + 1]).then_inc(gelu_done, 1)

            def between():
                act.wait_ge(gap_ready, 1)
                act.activation(rk[:, 1, :], rk[:, 0, :], ACT.Exp).then_inc(gap_exp, 1)
                expert_tiles(act, gelus)
            attention(act, body, between)

        @block.tensor
        def _(pe):
            pe.wait_ge(made, 2)

            def joint(i):
                for s in range(2):
                    pe.wait_ge(xts_ready, 2 * i + s + 1)
                    for t in range(TB):
                        tile = TB * (2 * i + s) + t
                        if some(tile - TB + 1):
                            pe.wait_ge(sq_ready, tile - TB + 1)
                        pe.matmul(psum[:, 2 + t, 0:WV0], xts[:, s, t * P:(t + 1) * P], wall[:, 0:WV0],
                                  start=True, stop=True).then_inc(joint_done, 1)

            def step(i):
                if known(i, 0):
                    pe.wait_ge(w_in, 48)
                else:
                    joint(i - 1)
                for s in range(2):
                    pe.wait_ge(xn_ready, 2 * i + s + 1)
                    if some(2 * i + s - 1):
                        pe.wait_ge(xts_ready, 2 * i + s - 1)
                    for t in range(TB):
                        mm = pe.transpose(psum[:, s, t * P:(t + 1) * P], xns[:, s, t, :], identf[:])
                    mm.then_inc(tr_done, 1)
                pe.wait_ge(wn_in, 32 * (i + 1))
                if some(2 * i):
                    pe.wait_ge(wt_ready, 2 * i)
                for c in range(MC):
                    mm = pe.transpose(psum[:, 6, c * P:(c + 1) * P], w1n[:, c, :], identf[:])
                mm.then_inc(wtr_done, 1)
                for c in range(MC):
                    mm = pe.transpose(psum[:, 7, c * P:(c + 1) * P], w2n[:, c * P:(c + 1) * P], identf[:])
                mm.then_inc(wtr_done, 1)
            stage_a(pe, step)
            joint(NB // 2 - 1)

            pe.wait_ge(b1_in, 16)
            pe.wait_ge(wt_ready, 2 * (NB // 2))
            pe.transpose(psum[:, 6, 0:E * MC], b1n[:], identf[0:E * MC, 0:E * MC]).then_inc(btr_done, 1)
            def project(b, t):
                tile = TB * b + t
                if t == 0:
                    pe.wait_ge(xt_in, 16 * (b + 1))
                    if some(b - 2):
                        pe.wait_ge(added, b - 2)
                if some(tile):
                    pe.wait_ge(proj_evac, tile)
                pe.matmul(ps_pa[:, 0:3 * D], xt[:, t * P:(t + 1) * P], wall[:, E:WEND],
                          start=True, stop=True).then_inc(proj_done, 1)

            def turn_qk(b, q):
                m = NQ * b + q
                pe.wait_ge(dup_done, TB * (b + 1))
                if some(m):
                    pe.wait_ge(qk_evac, m)
                for side in range(2):
                    for t in range(TB):
                        src = dup[:, t, side, QH * q:QH * (q + 1), :].rearrange("p h c -> p (h c)")
                        mm = pe.transpose(ps_pb[:, side * N + t * P:side * N + (t + 1) * P], src, identh[:])
                mm.then_inc(qktr_done, 1)

            def scores(b, q, u):
                n = NQ * b + q
                if u == 0:
                    pe.wait_ge(qk_evac, n + 1)
                    pe.wait_ge(ks_in[q], 16 * QH * (b + 1))
                if some(UN * n + u - 1):
                    pe.wait_ge(exp_done, UN * n + u - 1)
                s = score[(q + u) % 2]
                if u < QH:
                    parts = [(u, *part) for part in PARTS]
                else:
                    parts = [(g, 2, g * 2 * P, 2 * P, 2 * P) for g in range(QH)]
                for g, kt, col, first, cols in parts:
                    mm = pe.matmul(s[:, col:col + cols], ks[:, g, q, kt * P:(kt + 1) * P],
                                   qks[:, q, 0, first:first + cols], start=True, stop=True)
                mm.then_inc(scored, 1)

            def weigh(n, q, parts):
                for i in parts:
                    kt, col, first, cols = PARTS[i] if i < 4 else (2, None, 2 * P, 2 * P)
                    if i == 0:
                        if some(n):
                            pe.wait_ge(o_evac, n)
                        pe.wait_ge(exp_done, UN * n + QH)
                    if i == 1:
                        pe.wait_ge(masked, QH // 2 * (n + 1))
                    if i == 4:
                        pe.wait_ge(masked2, n + 1)
                    for g in range(QH):
                        u, c = (g, col) if i < 4 else (QH, g * 2 * P)
                        h = QH * q + g
                        mm = pe.matmul(ps_o[32 * g:32 * g + DH + 1, first:first + cols], v[:, kt * H + h, :],
                                       prob[:, q % 2, u, c:c + cols], start=(i == 0), stop=(i == 4),
                                       skip_group_check=True)
                if parts[-1] == 4:
                    mm.then_inc(pv_done, 1)

            def turn_o(n):
                pe.wait_ge(o_evac, n + 1)
                for t in range(TB):
                    mm = pe.transpose(ps_pc[:, t * P:(t + 1) * P], osb[:, t * P:(t + 1) * P], identf[:])
                mm.then_inc(otr_done, 1)

            def turn_on(b):
                pe.wait_ge(norm_done, NQ * (b + 1))
                for t in range(TB):
                    mm = pe.transpose(ps_pc[:, t * P:(t + 1) * P], on[:, t, :], identf[:])
                mm.then_inc(ontr_done, 1)

            def out_project(b, projected):
                pe.wait_ge(ot_ready, b + 1)
                pe.wait_ge(proj_evac, projected)
                for t in range(TB):
                    mm = pe.matmul(ps_pa[:, t * D:(t + 1) * D], ot[:, t * P:(t + 1) * P], wo[:],
                                   start=True, stop=True)
                mm.then_inc(outp_done, 1)

            pe.wait_ge(wv_in, 32)
            pe.wait_ge(sq_ready, T)
            pe.wait_ge(bt_ready, 1)
            for t in range(TB):
                project(0, t)
            turn_qk(0, 0)
            turn_qk(0, 1)
            pe.wait_ge(chosen, 1)
            flat_both = both[:].rearrange("p t e -> p (t e)")
            pe.matmul(ps_pc, before[:], flat_both, start=True, stop=True)
            pe.matmul(ps_o, ones[:], flat_both, start=True, stop=True).then_inc(counted, 1)
            pe.wait_ge(v_ready, 1)

            def body(b, second=False, last=False):
                if known(b, HALF):
                    pe.wait_ge(gelu_done, MC * FFN_TILES)
                    pe.wait_ge(ys_ready, FFN_TILES)
                for q in range(NQ):
                    n = NQ * b + q
                    scores(b, q, 0)
                    if not (known(b, 0) and q < 2):
                        if q == 2:
                            if some(b):
                                pe.wait_ge(ot_ready, b)
                        if some(n - 2):
                            pe.wait_ge(norm_done, n - 2)
                        turn_o(n - 2)
                    scores(b, q, 1)
                    before_this = not (known(b, 0) and q == 0)
                    if before_this:
                        if q == 1:
                            pe.wait_ge(v_ready, b + 1)
                            if known(b, 0):
                                pe.wait_ge(routed, 1)
                        weigh(n - 1, (q - 1) % NQ, [0])
                    scores(b, q, 2)
                    if before_this:
                        weigh(n - 1, (q - 1) % NQ, [1, 3])
                    if q == 0:
                        turn_qk(b, 2)
                    elif not last:
                        if q == 1:
                            project(b + 1, 0)
                        elif q == 2:
                            project(b + 1, 2)
                        else:
                            turn_qk(b + 1, 0)
                    if q == 3 and not known(b, 0):
                        out_project(b - 1, TB * (b + 1) if last else TB * (b + 2))
                    scores(b, q, 3)
                    if before_this:
                        weigh(n - 1, (q - 1) % NQ, [2, 4])
                    if q == 1 and not known(b, 0):
                        turn_on(b - 1)
                    scores(b, q, 4)
                    if q == 0:
                        turn_qk(b, 3)
                    elif not last:
                        if q == 1:
                            project(b + 1, 1)
                        elif q == 2:
                            project(b + 1, 3)
                        else:
                            turn_qk(b + 1, 1)

            def between():
                pe.wait_ge(exp_done, UN * NQ * HALF)
                pe.wait_ge(o_evac, NQ * HALF - 1)
                pe.wait_ge(proj_evac, TB * (HALF + 1))
                pe.wait_ge(qk_evac, NQ * HALF + 2)
                pe.wait_ge(norm_done, NQ * HALF - 2)
                pe.wait_ge(added, HALF - 1)

                def turn_x(k, s):
                    pe.wait_ge(xg_in[s], 8 * (k - s) + 16)
                    if some(k - 1):
                        pe.wait_ge(xgt_ready, k - 1)
                    for j in range(FJ):
                        mm = pe.transpose(psum[:, 4 + s, j * P:(j + 1) * P], xg[:, s, j, :], identf[:])
                    mm.then_inc(xgtr_done, 1)

                def hidden(k, s):
                    pe.wait_ge(xgt_ready, k + 1)
                    pe.wait_ge(w1_ready, k + 1)
                    if some(MC * (k - 1)):
                        pe.wait_ge(gelu_done, MC * (k - 1))
                    for c in range(MC):
                        mm = pe.matmul(psum[:, 2 * s + c // 2, (c % 2) * FT:(c % 2 + 1) * FT],
                                       ws[:, s, c * P:(c + 1) * P], xgt[:, s, :], start=True, stop=True)
                        if c % 2:
                            mm.then_inc(hid_done, 1)

                def outputs(k, s):
                    pe.wait_ge(w2_ready, k + 1)
                    pe.wait_ge(gelu_done, MC * (k + 1))
                    if some(k - 1):
                        pe.wait_ge(ys_ready, k - 1)
                    for j in range(FJ):
                        for c in range(MC):
                            mm = pe.matmul(psum[:, 6 + s, j * D:(j + 1) * D], hs[:, s, c, j * P:(j + 1) * P],
                                           ws[:, s, W2C + c * D:W2C + (c + 1) * D],
                                           start=(c == 0), stop=(c == MC - 1))
                    mm.then_inc(y_done, 1)

                turn_x(0, 0)

                def step(k, s):
                    if not isinstance(k, int) or k + 1 < FFN_TILES:
                        turn_x(k + 1, 1 - s)
                    hidden(k, s)
                    if not known(k, 0):
                        outputs(k - 1, 1 - s)
                expert_tiles(pe, step)
                outputs(FFN_TILES - 1, (FFN_TILES - 1) % 2)

            attention(pe, body, between)
            n = NQ * NB
            pe.wait_ge(norm_done, n - 2)
            turn_o(n - 2)
            weigh(n - 1, NQ - 1, [0, 1, 3, 2, 4])
            pe.wait_ge(norm_done, n - 1)
            turn_o(n - 1)
            turn_on(NB - 1)
            pe.wait_ge(added, NB - 1)
            out_project(NB - 1, TB * NB)

        @block.vector
        def _(dve):
            def sum_squares(i):
                for s in range(2):
                    b = 2 * i + s
                    dve.wait_ge(sq_ready, TB * (b + 1))
                    src = sq[:, s].rearrange("p t (h d) -> p t h d", d=DH)
                    dve.tensor_reduce(norms[:, at(TB * b, TB), :], src, AX.X, ALU.add).then_inc(ss_ready, 1)

            def step(i):
                for s in range(2):
                    dve.wait_ge(xs_in[s], 16 * (i + 1))
                    if some(2 * i + s - 1):
                        dve.wait_ge(mv_ready, 2 * i + s - 1)
                    for t in range(TB):
                        ins = dve.bn_stats(bst[:, s, t, :], xs[:, s, t, :])
                    ins.then_inc(stats, 1)
                for s in range(2):
                    count = counted_by(dve, 2 * i + s + 1)
                    dve.wait_ge(made, 1)
                    dve.wait_ge(stats, count)
                    if some(2 * i + s - 1):
                        dve.wait_ge(xn_ready, 2 * i + s - 1)
                    for t in range(TB):
                        ins = dve.bn_aggr(mv[:, s, t, :], bst[:, s, t, :])
                    ins.then_inc(r_step, 1)
                for s in range(2):
                    dve.wait_ge(r_step, 2 * i + 2)
                    if some(2 * i + s - 1):
                        dve.wait_ge(std_ready, 2 * i + s - 1)
                    dve.tensor_scalar(mv[:, s, :, 1], mv[:, s, :, 1], LN_EPS, None, ALU.add).then_inc(mv_ready, 1)
                for s in range(2):
                    dve.wait_ge(std_ready, 2 * i + s + 1)
                    dve.reciprocal(rstd[:, s], std[:, s]).then_inc(rstd_ready, 1)
                    dve.wait_ge(rstd_ready, 2 * i + s + 1)
                    if some(2 * i + s - 1):
                        dve.wait_ge(tr_done, 2 * i + s - 1)
                    if some(16 * i):
                        dve.wait_ge(rows_out[s], 16 * i)
                    for t in range(TB):
                        ins = dve.tensor_scalar(xns[:, s, t, :], xs[:, s, t, :], mv[:, s, t, 0:1],
                                                rstd[:, s, t:t + 1], ALU.subtract, ALU.mult)
                    ins.then_inc(xn_ready, 1)
                if not known(i, 0):
                    sum_squares(i - 1)
            stage_a(dve, step)
            sum_squares(NB // 2 - 1)
            dve.wait_ge(ss_ready, NB)
            dve.tensor_scalar(norms[:], norms[:], NORM_EPS ** 2, None, ALU.max).then_inc(floored, 1)
            dve.wait_ge(made, 3)
            dve.wait_ge(btr_done, 1)
            dve.tensor_copy(wexp[:, :, B1C:W2C], psum[:, 6, 0:E * MC].rearrange("p (e c) -> p e c", e=E))\
                .then_inc(bt_ready, 1)

            steps = NB

            def next_step():
                nonlocal steps
                steps += 1
                return steps

            def prepare(b, t):
                tile = TB * b + t
                if t == 0:
                    if some(tile):
                        dve.wait_ge(qn_done, tile)
                    dve.reciprocal(rnb[:], norms[:, at(TB * b, TB), :]).then_inc(rn_done, 1)
                    dve.wait_ge(rn_done, b + 1)
                    if some(NQ * b):
                        dve.wait_ge(qktr_done, NQ * b)
                    if some(b):
                        dve.wait_ge(v_ready, b)
                dve.wait_ge(proj_done, tile + 1)
                if some(tile):
                    dve.wait_ge(dup_done, tile)
                scale = rnb[:, t, :].rearrange("p (h a) -> p h a", a=1).broadcast_to([P, NQK, DH])
                dve.tensor_tensor(qn[:], ps_pa[:, 0:2 * D].rearrange("p (h d) -> p h d", d=DH), scale, ALU.mult)\
                    .then_inc(qn_done, 1)
                dve.tensor_copy(vn[:, t * H:(t + 1) * H, :], ps_pa[:, 2 * D:3 * D].rearrange("p (h d) -> p h d", d=DH))\
                    .then_inc(proj_evac, 1)
                dve.wait_ge(qn_done, tile + 1)
                q_to = dup[:, t, 0].rearrange("p h (a b d) -> p h a b d", a=2, b=2)
                k_to = dup[:, t, 1].rearrange("p h (a b d) -> p h a b d", a=2, b=2)

                def twice(ap):
                    return ap.rearrange("p h (a d) -> p h a d", a=1).broadcast_to([P, H, 2, DH])
                q32, k32 = twice(qn[:, 0:H, :]), twice(qn[:, H:NQK, :])
                dve.tensor_copy(q_to[:, :, :, 0, :], q32)
                dve.tensor_copy(k_to[:, :, 0, :, :], k32).then_inc(hi_done, 1)
                dve.wait_ge(hi_done, tile + 1)
                dve.tensor_tensor(q_to[:, :, :, 1, :], q32, q_to[:, :, :, 0, :], ALU.subtract)
                dve.tensor_tensor(k_to[:, :, 1, :, :], k32, k_to[:, :, 0, :, :], ALU.subtract).then_inc(dup_done, 1)

            def copy_qk(b, q):
                m = NQ * b + q
                dve.wait_ge(qktr_done, m + 1)
                if some(UN * (m - NQ + 1)):
                    dve.wait_ge(scored, UN * (m - NQ + 1))
                dve.tensor_copy(qks[:, q].rearrange("p a n -> p (a n)"), ps_pb).then_inc(qk_evac, 1)

            def copy_v(b):
                dve.wait_ge(proj_evac, TB * (b + 1))
                if some(NQ * b):
                    dve.wait_ge(pv_done, NQ * b)
                dve.tensor_copy(v[:, :, 0:DH], vn[:]).then_inc(v_ready, 1)

            dve.wait_ge(norms_ready, 1)
            for t in range(TB):
                prepare(0, t)
            copy_v(0)
            copy_qk(0, 0)
            copy_qk(0, 1)

            def by_expert(ap):
                return ap.rearrange("p (t a) -> p t a", a=1).broadcast_to([P, T, E])

            back_t = back[:].rearrange("p (a e) -> p a e", a=1).broadcast_to([P, T, E])
            src = logits[:]
            for c in range(TOPK):
                dve.tensor_reduce(top[:, c], src, AX.X, ALU.max).then_inc(r_step, 1)
                dve.wait_ge(r_step, next_step())
                dve.tensor_tensor(tmp, src, by_expert(top[:, c]), ALU.is_equal).then_inc(r_step, 1)
                dve.wait_ge(r_step, next_step())
                dve.tensor_tensor(tmp, tmp, back_t, ALU.mult).then_inc(r_step, 1)
                dve.wait_ge(r_step, next_step())
                dve.tensor_reduce(rk[:, c], tmp, AX.X, ALU.max).then_inc(r_step, 1)
                dve.wait_ge(r_step, next_step())
                dve.tensor_tensor(hot[:, c], tmp, by_expert(rk[:, c]), ALU.is_equal).then_inc(r_step, 1)
                dve.wait_ge(r_step, next_step())
                if c == 0:
                    dve.tensor_scalar(tmp, hot[:, 0], -3.0e38, None, ALU.mult).then_inc(r_step, 1)
                    dve.wait_ge(r_step, next_step())
                    dve.tensor_tensor(lg2, logits[:], tmp, ALU.add).then_inc(r_step, 1)
                    dve.wait_ge(r_step, next_step())
                    src = lg2
            dve.tensor_tensor(both[:], hot[:, 0], hot[:, 1], ALU.add).then_inc(chosen, 1)
            dve.tensor_tensor(rk[:, 0], top[:, 1], top[:, 0], ALU.subtract).then_inc(r_step, 1)
            dve.wait_ge(r_step, next_step())
            dve.sem_inc(gap_ready, 1)
            dve.memset(pre, 0.0).then_inc(r_step, 1)
            dve.wait_ge(r_step, next_step())
            dve.wait_ge(counted, 1)
            totals = ps_o.rearrange("p (t e) -> p t e", e=E)
            within = ps_pc.rearrange("p (t e) -> p t e", e=E)
            dve.tensor_copy(pre[:, 0, T // 2:, :], totals).then_inc(r_step, 1)
            dve.wait_ge(r_step, next_step())
            side, shift = 0, 1
            while shift < T:
                dve.tensor_tensor(pre[:, 1 - side, T // 2:, :], pre[:, side, T // 2:, :],
                                  pre[:, side, T // 2 - shift:T // 2 + T - shift, :], ALU.add).then_inc(r_step, 1)
                dve.wait_ge(r_step, next_step())
                side, shift = 1 - side, 2 * shift
            incl = pre[:, side, T // 2:, :]
            dve.tensor_scalar(cnti[:, 0], incl[:, T - 1, :], float(FT - 1), None, ALU.add).then_inc(r_step, 1)
            dve.wait_ge(r_step, next_step())
            dve.tensor_scalar(cnti[:, 1], cnti[:, 0], FSH, FSH, ALU.logical_shift_right, ALU.logical_shift_left)\
                .then_inc(r_step, 1)
            dve.wait_ge(r_step, next_step())
            dve.tensor_copy(cnt[:, 1, E:], cnti[:, 1]).then_inc(r_step, 1)
            dve.wait_ge(r_step, next_step())
            level, shift = 1, 1
            while shift < E:
                dve.tensor_tensor(cnt[:, level + 1, E:], cnt[:, level, E:], cnt[:, level, E - shift:2 * E - shift],
                                  ALU.add).then_inc(r_step, 1)
                dve.wait_ge(r_step, next_step())
                level, shift = level + 1, 2 * shift
            ends = cnt[:, level, E:]
            dve.tensor_tensor(cnt[:, 0, E:], ends, cnt[:, 1, E:], ALU.subtract).then_inc(r_step, 1)
            dve.wait_ge(r_step, next_step())
            def both_rows(ap):
                return ap.rearrange("p (a e) -> p a e", a=1).broadcast_to([P, FJ, E])

            def pad(i):
                return padf[:, i].rearrange("p (j e) -> p j e", j=FJ)
            dve.tensor_tensor(padf[:, 1, 0:E], cnt[:, 0, E:], incl[:, T - 1, :], ALU.add).then_inc(r_step, 1)
            dve.wait_ge(r_step, next_step())
            dve.tensor_tensor(pad(2), pad(0), both_rows(padf[:, 1, 0:E]), ALU.add).then_inc(r_step, 1)
            dve.wait_ge(r_step, next_step())
            dve.tensor_tensor(pad(3), pad(2), both_rows(ends), ALU.is_lt).then_inc(r_step, 1)
            dve.wait_ge(r_step, next_step())
            dve.tensor_tensor(padf[:, 1], padf[:, 2], padf[:, 4], ALU.subtract).then_inc(r_step, 1)
            dve.wait_ge(r_step, next_step())
            dve.tensor_tensor(padf[:, 2], padf[:, 1], padf[:, 3], ALU.mult).then_inc(r_step, 1)
            dve.wait_ge(r_step, next_step())
            dve.tensor_tensor(pads[:], padf[:, 2], padf[:, 4], ALU.add).then_inc(r_step, 1)
            dve.wait_ge(r_step, next_step())
            dve.tensor_scalar(tile_f[:, 0], starts[:], ends[:, 0:1], None, ALU.is_ge).then_inc(r_step, 1)
            dve.wait_ge(r_step, next_step())
            for e in range(1, E - 1):
                dve.scalar_tensor_tensor(out=tile_f[:, e % 2], in0=starts[:], scalar=ends[:, e:e + 1],
                                         in1=tile_f[:, (e - 1) % 2], op0=ALU.is_ge, op1=ALU.add).then_inc(r_step, 1)
                dve.wait_ge(r_step, next_step())
            dve.tensor_copy(tile_i[:], tile_f[:, (E - 2) % 2]).then_inc(r_step, 1)
            dve.wait_ge(r_step, next_step())
            dve.tensor_tensor(tmp, incl, totals, ALU.subtract).then_inc(r_step, 1)
            dve.wait_ge(r_step, next_step())
            dve.tensor_tensor(lg2, tmp, within, ALU.add).then_inc(r_step, 1)
            dve.wait_ge(r_step, next_step())
            base = cnt[:, 0:1, E:].broadcast_to([P, T, E])
            dve.tensor_tensor(tmp, lg2, base, ALU.add).then_inc(r_step, 1)
            dve.wait_ge(r_step, next_step())
            for c in range(TOPK):
                dve.tensor_tensor(lg2, hot[:, c], tmp, ALU.mult).then_inc(r_step, 1)
                dve.wait_ge(r_step, next_step())
                dve.tensor_reduce(slotf[:, c], lg2, AX.X, ALU.add).then_inc(r_step, 1)
                dve.wait_ge(r_step, next_step())
                dve.tensor_copy(slots[:, :, c], slotf[:, c]).then_inc(r_step, 1)
                dve.wait_ge(r_step, next_step())
            dve.memset(ps_o, 0.0).then_inc(r_step, 1)
            dve.wait_ge(r_step, next_step())
            dve.sem_inc(routed, 1)

            def mask2(n, q):
                dve.wait_ge(exp_done, UN * (n + 1))
                p = prob[:, q % 2, QH, :].rearrange("p (g c) -> p g c", g=QH)[:, :, 0:P]
                dve.tensor_tensor(p, p, causal[:].rearrange("p (a c) -> p a c", a=1).broadcast_to([P, QH, P]), ALU.mult)\
                    .then_inc(masked2, 1)

            def divide(n, q):
                dve.wait_ge(otr_done, n + 1)
                o = ps_pc.rearrange("p (t g c) -> p t g c", t=TB, g=QH)
                if some(n):
                    dve.wait_ge(norm_done, n)
                dve.reciprocal(rs[:], o[:, :, :, DH]).then_inc(rs_done, 1)
                dve.wait_ge(rs_done, n + 1)
                to = on.rearrange("p t (q g d) -> p t q g d", q=NQ, g=QH)[:, :, q]
                dve.tensor_tensor(to, o[:, :, :, 0:DH],
                                  rs[:].rearrange("p t (g a) -> p t g a", a=1).broadcast_to([P, TB, QH, DH]), ALU.mult)\
                    .then_inc(norm_done, 1)

            def copy_o(n):
                dve.wait_ge(pv_done, n + 1)
                if some(n):
                    dve.wait_ge(otr_done, n)
                dve.tensor_copy(osb, ps_o).then_inc(o_evac, 1)

            def add_attention(b, combines):
                dve.wait_ge(outp_done, b + 1)
                if some(combines):
                    dve.wait_ge(combined, combines)
                if known(b, 0):
                    dve.wait_ge(acc_in, 16)
                a = acc[:, at(TB * b, TB), :]
                dve.tensor_tensor(a, ps_pa.rearrange("p (t d) -> p t d", t=TB), a, ALU.add).then_inc(added, 1)

            def combine(b, j, adds):
                k = 2 * (b - HALF) + j
                dve.wait_ge(moved[j], 16 * TB * TOPK * (b + 1))
                dve.wait_ge(added, adds)
                for c in range(TOPK):
                    if some(TB * TOPK * k + TB * c):
                        dve.wait_ge(combined, TB * TOPK * k + TB * c)
                    for t in range(TB):
                        a = acc[:, at(TB * k + t), :]
                        r = rows[:, j, c, t:t + 1, :]
                        dve.scalar_tensor_tensor(out=a, in0=r, scalar=gate[:, c, at(TB * k + t)], in1=a,
                                                 op0=ALU.mult, op1=ALU.add).then_inc(combined, 1)

            def body(b, second=False, last=False):
                each = TB * TOPK
                for q in range(NQ):
                    n = NQ * b + q
                    if not (known(b, 0) and q == 0):
                        mask2(n - 1, (q - 1) % NQ)
                    if not (known(b, 0) and q < 2):
                        if q == 2:
                            if some(b):
                                dve.wait_ge(ontr_done, b)
                        divide(n - 2, (q - 2) % NQ)
                    if q == 0:
                        copy_qk(b, 2)
                    elif not last:
                        if q == 1:
                            prepare(b + 1, 0)
                        elif q == 2:
                            prepare(b + 1, 2)
                        else:
                            copy_qk(b + 1, 0)
                    if q == 3 and not known(b, 0):
                        add_attention(b - 1, each * (2 * (b - HALF)) if second else 0)
                    if not (known(b, 0) and q == 0):
                        copy_o(n - 1)
                    if q == 0 and not known(b, 0):
                        copy_v(b)
                    if q == 1 and not known(b, 0):
                        dve.wait_ge(ontr_done, b)
                        if some(b - 1):
                            dve.wait_ge(outp_done, b - 1)
                        dve.tensor_copy(ot, ps_pc).then_inc(ot_ready, 1)
                    if q == 0:
                        copy_qk(b, 3)
                    elif not last:
                        if q == 1:
                            prepare(b + 1, 1)
                        elif q == 2:
                            prepare(b + 1, 3)
                        else:
                            copy_qk(b + 1, 1)
                    if second and q == 1 and not known(b, HALF):
                        combine(b - 1, 1, b - 1)
                    if second and q == 3:
                        combine(b, 0, b)

            def between():
                dve.wait_ge(acc_in, 32)
                dve.wait_ge(gap_exp, 1)
                dve.tensor_scalar(rk[:, 0], rk[:, 1], 1.0, None, ALU.add).then_inc(r_step, 1)
                dve.wait_ge(r_step, next_step())
                dve.reciprocal(gate[:, 0], rk[:, 0]).then_inc(r_step, 1)
                dve.wait_ge(r_step, next_step())
                dve.tensor_tensor(gate[:, 1], gate[:, 0], rk[:, 1], ALU.mult).then_inc(r_step, 1)
                dve.wait_ge(r_step, next_step())
                dve.wait_ge(b2_in, 16)
                dve.wait_ge(bt_ready, 1)
                dve.wait_ge(wt_ready, 2 * (NB // 2))
                dve.wait_ge(pv_done, NQ * HALF - 1)

                def copy_w1(k, s):
                    e = dve.value_load(tile_i[0:1, at(k)], min_val=0, max_val=E - 1)
                    if some(k - 1):
                        dve.wait_ge(hid_done, 2 * (k - 1))
                        dve.wait_ge(gelu_done, MC * (k - 1))
                    dve.tensor_copy(ws[:, s:s + 1, 0:W2C], wexp[:, at(e), 0:W2C]).then_inc(w1_ready, 1)
                    return e

                def copy_w2(k, s, e):
                    if some(k - 1):
                        dve.wait_ge(y_done, k - 1)
                        dve.wait_ge(ys_ready, k - 1)
                    dve.tensor_copy(ws[:, s:s + 1, W2C:WX], wexp[:, at(e), W2C:WX]).then_inc(w2_ready, 1)

                def copy_x(k, s):
                    dve.wait_ge(xgtr_done, k + 1)
                    if some(2 * (k - 1)):
                        dve.wait_ge(hid_done, 2 * (k - 1))
                    dve.tensor_copy(xgt[:, s, :], psum[:, 4 + s, 0:FT]).then_inc(xgt_ready, 1)

                def copy_y(k, s):
                    dve.wait_ge(y_done, k + 1)
                    if some(8 * (k - s)):
                        dve.wait_ge(y_out[s], 8 * (k - s))
                    bias = ws[:, s:s + 1, B2C:WX].broadcast_to([P, FJ, D])
                    dve.tensor_tensor(ys[:, s], psum[:, 6 + s, 0:FT].rearrange("p (j d) -> p j d", j=FJ), bias, ALU.add)\
                        .then_inc(ys_ready, 1)

                e = copy_w1(0, 0)
                copy_w2(0, 0, e)
                copy_x(0, 0)

                def step(k, s):
                    more = not isinstance(k, int) or k + 1 < FFN_TILES
                    if more:
                        e = copy_w1(k + 1, 1 - s)
                        copy_x(k + 1, 1 - s)
                    if not known(k, 0):
                        copy_y(k - 1, 1 - s)
                    if more:
                        copy_w2(k + 1, 1 - s, e)
                expert_tiles(dve, step)
                copy_y(FFN_TILES - 1, (FFN_TILES - 1) % 2)

            attention(dve, body, between)
            n = NQ * NB
            mask2(n - 1, NQ - 1)
            divide(n - 2, NQ - 2)
            copy_o(n - 1)
            divide(n - 1, NQ - 1)
            dve.wait_ge(ontr_done, NB)
            dve.wait_ge(outp_done, NB - 1)
            dve.tensor_copy(ot, ps_pc).then_inc(ot_ready, 1)
            combine(NB - 1, 1, NB - 1)
            add_attention(NB - 1, 2 * TB * TOPK * HALF)


_INS = ["L0_attn_x", "L0_attn_Wq", "L0_attn_Wk", "L0_attn_Wv", "L0_attn_Wo", "L0_ffn_Wr", "L0_ffn_W1", "L0_ffn_b1",
        "L0_ffn_W2", "L0_ffn_b2"]


def kernel(**inputs):
    import numpy as _np
    import concourse.bacc as _bacc
    from concourse.bass_utils import run_bass_kernel_spmd as _run

    nc = _bacc.Bacc("TRN2", target_bir_lowering=False, num_devices=1)
    arrays, args = {}, []
    for name in _INS:
        a = _np.ascontiguousarray(inputs[name])
        arrays[f"in_{name}"] = a
        args.append(nc.dram_tensor(f"in_{name}", a.shape, mybir.dt.from_np(a.dtype), kind="ExternalInput").ap())
    shape = arrays["in_L0_attn_x"].shape
    args.append(nc.dram_tensor("out_0", shape, F32, kind="ExternalOutput").ap())
    build(nc, *args)
    r = _run(nc, [arrays], core_ids=[0])
    return r.results[0]["out_0"]
```

```python
from contextlib import ExitStack

import concourse.bass as bass
from concourse import mybir

P = 128
ALU = mybir.AluOpType
ACT = mybir.ActivationFunctionType
AX = mybir.AxisListType
F32 = mybir.dt.float32
F16 = mybir.dt.float16
I32 = mybir.dt.int32


def build(nc, x, Wq, Wk, Wv, Wo, Wr, W1, b1, W2_, b2, out):
    NB, N, D = x.shape
    E, M, _ = W1.shape
    H, DH = 16, D // 16
    TB = N // P
    T = NB * TB
    QH, NQ = 4, H // 4
    MC = M // P
    TOPK = 2
    FJ = 2
    FT = FJ * P
    FSH = FT.bit_length() - 1
    FFN_TILES = (TOPK * NB * N + E * (FT - 1)) // FT
    SLOTS = FFN_TILES * FT
    HALF = NB // 2
    SCALE, NORM_EPS, LN_EPS = 8.0, 1e-12, 1e-5
    UP = 64.0
    NQK = 2 * H
    WV0, WEND = E + 2 * D, E + 3 * D
    B1C, W2C, B2C = M, M + MC, 2 * M + MC
    WX = B2C + D
    ST = 4 * TB
    SELECT = 11
    UN = 5
    UW = 1024
    PARTS = [(0, 0, P, N - P), (0, N - P, 0, P), (3, N, 3 * P, P), (1, N + P, P, N - P)]
    DIAG = N - P

    with ExitStack() as ctx:
        def sb(name, shape, dt=F32):
            return ctx.enter_context(nc.sbuf_tensor(name, shape, dt))

        def sem(name):
            return ctx.enter_context(nc.semaphore(name))

        def sems(names):
            return [sem(n) for n in names.split()]

        def pair(name):
            return [sem(f"{name}{s}") for s in range(2)]

        def dram(name, shape, dt=F32):
            return nc.dram_tensor(name, shape, dt).ap()

        xn_rows = dram("xn_rows", [NB, N, D])
        xn_cols = dram("xn_cols", [NB, D, N])
        slot_x = dram("slot_x", [SLOTS + E * FT, D])
        slot_y = dram("slot_y", [SLOTS, D])

        identf = sb("identf", [P, P])
        identh = sb("identh", [P, P], F16)
        before = sb("before", [P, P], F16)
        ones = sb("ones", [P, P], F16)
        causal = sb("causal", [P, P])
        zeros = sb("zeros", [P, D])
        back = sb("back", [P, E])
        starts = sb("starts", [P, FFN_TILES])
        consti = sb("consti", [P, E + FFN_TILES], I32)
        residue = sb("residue", [P, E], F16)
        wall = sb("wall", [P, WEND])
        wo = sb("wo", [P, D])
        wexp = sb("wexp", [P, E, WX])
        b1n = sb("b1n", [E * MC, P])

        acc = sb("acc", [P, T, D])

        xs = sb("xs", [P, 2, 2, TB, D])
        bst = sb("bst", [P, 2, TB, 6])
        mv = sb("mv", [P, 2, TB, 2])
        std = sb("std", [P, 2, TB])
        rstd = sb("rstd", [P, 2, TB])
        xns = sb("xns", [P, 2, TB, D])
        xts = sb("xts", [P, 2, 2, N])
        logits = sb("logits", [P, T, E])
        norms = sb("norms", [P, T, NQK])
        totals = xs[:, 0, 0].rearrange("p t d -> p (t d)").bitcast(F16)[:, 0:T * E].rearrange("p (c n) -> p c n", n=P)

        prob = sb("prob", [P, 2, UN, UW])
        flat_prob = prob[:].rearrange("p a u w -> p (a u w)")
        w1n = flat_prob[:, 0:M].rearrange("p (c d) -> p c d", c=MC)
        w2n = flat_prob[:, M:2 * M]
        sq = flat_prob[:, 2 * M:2 * M + 2 * TB * 2 * D].rearrange("p (s t c) -> p s t c", s=2, t=TB)

        hot = sb("hot", [P, TOPK, T, E])
        both = sb("both", [P, T, E], F16)
        spent = sb("spent", [P, ST, E])
        mark = sb("mark", [P, ST, E])
        top = sb("top", [P, TOPK, ST])
        rank = sb("rank", [P, TOPK, ST])
        gap = sb("gap", [P, T])
        gapx = sb("gapx", [P, 2, T])
        cnt = sb("cnt", [P, 5, 2 * E])
        cnti = sb("cnti", [P, 2, E], I32)
        slots = sb("slots", [P, T, TOPK], I32)
        gate = sb("gate", [P, TOPK, T])
        tile_f = sb("tile_f", [P, 2, FFN_TILES])
        tile_i = sb("tile_i", [P, FFN_TILES], I32)
        lastf = sb("lastf", [P, 4, E])
        last_i = sb("last_i", [P, E], I32)

        xt = sb("xt", [P, N])
        rnb = sb("rnb", [P, TB, NQK])
        qn = sb("qn", [P, NQK, DH])
        dup = sb("dup", [P, TB, 2, H, 4 * DH], F16)
        qks = sb("qks", [P, NQ, 2, N], F16)
        ks = sb("ks", [P, QH, NQ, N], F16)
        vn = sb("vn", [P, TB * H, DH])
        v = sb("v", [P, TB * H, DH + 1])
        rs = sb("rs", [P, TB, QH])
        turn = sb("turn", [P, 3 * N])
        osb = turn[:, 0:N]
        on = turn[:, N:2 * N].rearrange("p (t d) -> p t d", t=TB)
        ot = turn[:, 2 * N:3 * N]
        later = turn[:, 0:T * E * T * E // P // 2].bitcast(F16).rearrange("p (c t e) -> p c t e", t=T, e=E)

        idx = sb("idx", [P, 2, TB, TOPK], I32)
        rows = sb("rows", [P, 2, TOPK, TB, D])
        mine = rows[:, 0, 1].rearrange("p t (u e) -> p (t u) e", e=E)
        place = rows[:, 1, 1].rearrange("p t (u e) -> p (t u) e", e=E)
        flat_rows = rows[:].rearrange("p a c t d -> p (a c t d)")
        half_sums = flat_rows[:, 0:512].rearrange("p (t h d) -> p t h d", t=TB, h=NQK)
        quarter_sums = flat_rows[:, 512:768].rearrange("p (t h d) -> p t h d", t=TB, h=NQK)
        sums = flat_rows[:, 1024:1280].rearrange("p (s t h) -> p s t h", s=2, t=TB)
        xg = flat_rows[:, 0:2 * FT].rearrange("p (s j d) -> p s j d", s=2, j=FJ)
        xgt = flat_rows[:, 2 * FT:4 * FT].rearrange("p (s n) -> p s n", s=2)
        ys = flat_rows[:, 4 * FT:6 * FT].rearrange("p (s j d) -> p s j d", s=2, j=FJ)
        hs = flat_prob[:, 0:2 * MC * FT].rearrange("p (s c n) -> p s c n", s=2, c=MC)
        ws = flat_prob[:, 2 * MC * FT:2 * MC * FT + 2 * WX].rearrange("p (s w) -> p s w", s=2)
        assert 2 * MC * FT + 2 * WX <= UN * UW and D == P and NB * TB * E == 512

        psum = ctx.enter_context(nc.psum_tensor("psum", [P, 8, 512], F32))
        score = [psum[:, 2 * s:2 * s + 2, :].rearrange("p a b -> p (a b)") for s in range(2)]
        ps_o, ps_pa, ps_pc = psum[:, 4, :], psum[:, 5, :], psum[:, 7, :]
        ps_pb = psum[:, 6, :].bitcast(F16)

        made, zero_made = sems("made zero_made")
        w_in, wv_in, acc_in, b1_in, b2_in, wn_in = sems("w_in wv_in acc_in b1_in b2_in wn_in")
        rows_out = pair("rows_out")
        xs_in, cols_out = [pair("xs_in0"), pair("xs_in1")], [pair("cols_out0"), pair("cols_out1")]
        stats, mv_ready, std_ready, rstd_ready, xn_ready = sems("stats mv_ready std_ready rstd_ready xn_ready")
        tr_done, xts_ready, joint_done, sq_ready, ss_ready = sems("tr_done xts_ready joint_done sq_ready ss_ready")
        norms_ready, zeroed, padded, halves, sel, selected = sems("norms_ready zeroed padded halves sel selected")
        wtr_done, wt_ready, btr_done, bt_ready = sems("wtr_done wt_ready btr_done bt_ready")
        r_step, counted, totals_read, placed = sems("r_step counted totals_read placed")
        lasts_ready, routed = sems("lasts_ready routed")
        residue_ready, later_ready = sems("residue_ready later_ready")
        gap_exp, = sems("gap_exp")
        xt_in, proj_done, rn_done, qn_done, proj_evac = sems("xt_in proj_done rn_done qn_done proj_evac")
        hi_done, dup_done, qktr_done, qk_evac = sems("hi_done dup_done qktr_done qk_evac")
        ks_in = [sem(f"ks_in{q}") for q in range(NQ)]
        scored, exp_done, masked, masked2 = sems("scored exp_done masked masked2")
        v_ready, pv_done, o_evac, otr_done = sems("v_ready pv_done o_evac otr_done")
        rs_done, norm_done, ontr_done, ot_ready = sems("rs_done norm_done ontr_done ot_ready")
        outp_done, added, idx_ready, combined, stored = sems("outp_done added idx_ready combined stored")
        rows_in, moved, xg_in, y_out = pair("rows_in"), pair("moved"), pair("xg_in"), pair("y_out")
        xgtr_done, xgt_ready, w1_ready, w2_ready, hid_done = sems("xgtr_done xgt_ready w1_ready w2_ready hid_done")
        gelu_done, y_done, ys_ready = sems("gelu_done y_done ys_ready")

        block = ctx.enter_context(nc.Block())

        def some(count):
            return not isinstance(count, int) or count > 0

        def counted_by(eng, count):
            return count if isinstance(count, int) else eng.to_reg(count)

        def known(i, value):
            return isinstance(i, int) and i == value

        def at(i, n=1):
            return slice(i, i + n) if isinstance(i, int) else bass.ds(i, n)

        def batch_rows(t, b):
            return t.rearrange("b (t p) d -> p (b t) d", p=P)[:, at(TB * b, TB), :]

        def batch_cols(b):
            return xn_cols.rearrange("b d n -> d b n")[:, at(b), :].rearrange("d b n -> d (b n)")

        def tile_rows(t, k):
            return t.rearrange("(u p) d -> p u d", p=P)[:, at(FJ * k, FJ), :]

        def stage_a(eng, step):
            for i in range(4):
                step(i, i % 2, i // 2)
            with eng.Fori(2, NB // 4 - 1) as j:
                step(2 * j, 0, j)
                step(2 * j + 1, 1, j)
            for i in range(NB // 2 - 2, NB // 2):
                step(i, i % 2, i // 2)

        def attention(eng, body, between):
            body(0)
            body(1)
            with eng.Fori(2, HALF - 1) as b:
                body(b)
            body(HALF - 1)
            between()
            body(HALF, second=True)
            with eng.Fori(HALF + 1, NB - 2) as b:
                body(b, second=True)
            body(NB - 2, second=True)
            body(NB - 1, second=True, last=True)

        def expert_tiles(eng, step):
            for k in range(4):
                step(k, k % 2)
            with eng.Fori(2, FFN_TILES // 2 - 1) as i:
                step(2 * i, 0)
                step(2 * i + 1, 1)
            for k in range(2 * (FFN_TILES // 2 - 1), FFN_TILES):
                step(k, k % 2)

        @block.sync
        def _(sp):
            def load_x(i, par):
                for s in range(2):
                    if some(2 * i + s - 3):
                        sp.wait_ge(xn_ready, 2 * i + s - 3)
                    sp.dma_start(xs[:, par, s], batch_rows(x, 2 * i + s)).then_inc(xs_in[par][s], 16)

            def load_weights(i):
                if some(2 * i):
                    sp.wait_ge(wtr_done, 2 * i)
                w1_e = W1.rearrange("e (c m) d -> m (e c) d", m=P)[:, at(MC * i, MC), :]
                sp.dma_start(w1n, w1_e).then_inc(wn_in, 16)
                w2_e = W2_.rearrange("e d m -> d e m")[:, at(i), :].rearrange("d e m -> d (e m)")
                sp.dma_start(w2n, w2_e).then_inc(wn_in, 16)

            def store(i, par):
                for s in range(2):
                    sp.wait_ge(xn_ready, 2 * i + s + 1)
                    sp.dma_start(batch_rows(xn_rows, 2 * i + s), xns[:, s]).then_inc(rows_out[s], 16)
                for s in range(2):
                    sp.wait_ge(xts_ready, 2 * i + s + 1)
                    sp.dma_start(batch_cols(2 * i + s), xts[:, par, s]).then_inc(cols_out[par][s], 16)

            def step(i, par, j):
                if not known(i, 0):
                    store(i - 1, 1 - par)
                load_weights(i)
                if not (known(i, NB // 2 - 2) or known(i, NB // 2 - 1)):
                    load_x(i + 2, par)
            load_x(0, 0)
            sp.dma_start(wall[:, 0:E], Wr.rearrange("e d -> d e"), allow_slow_non_contiguous=True).then_inc(w_in, 16)
            sp.dma_start(wall[:, E:E + D], Wq).then_inc(w_in, 16)
            sp.dma_start(wall[:, E + D:WV0], Wk).then_inc(w_in, 16)
            load_x(1, 1)
            sp.dma_start(wall[:, WV0:WEND], Wv).then_inc(wv_in, 16)
            sp.dma_start(wo[:], Wo).then_inc(wv_in, 16)
            stage_a(sp, step)
            def load_xt(b):
                if some(TB * b):
                    sp.wait_ge(proj_done, TB * b)
                sp.dma_start(xt[:], batch_cols(b)).then_inc(xt_in, 16)

            sp.wait_ge(cols_out[0][0], 16 * (NB // 4))
            load_xt(0)
            store(NB // 2 - 1, 1)
            sp.dma_start(b1n[:], b1.rearrange("e (c m) -> (e c) m", m=P)).then_inc(b1_in, 16)
            b2_all = b2.rearrange("e d -> (e d)").rearrange("(a e d) -> a e d", a=1, e=E).broadcast_to([P, E, D])
            sp.dma_start(wexp[:, :, B2C:WX], b2_all).then_inc(b2_in, 16)

            sp.wait_ge(zero_made, 1)
            spare = slot_x.rearrange("(u p) d -> p u d", p=P)[:, TOPK * T:SLOTS // P, :]
            nothing = zeros[:].rearrange("p (a d) -> p a d", a=1).broadcast_to([P, SLOTS // P - TOPK * T, D])
            sp.dma_start(spare, nothing).then_inc(zeroed, 16)

            def spread_k(m, q):
                sp.wait_ge(qk_evac, m + 1)
                for g in range(QH):
                    r = slice(32 * g, 32 * g + 32)
                    sp.dma_start(ks[r, g, q, :], qks[r, q, 1, :]).then_inc(ks_in[q], 16)

            for s in range(2):
                for par in range(2):
                    sp.wait_ge(cols_out[par][s], 16 * (NB // 4))
                sp.wait_ge(rows_out[s], 16 * (NB // 2))
            sp.wait_ge(made, 4)
            def load_rows(b, j):
                if some(16 * TB * TOPK * b):
                    sp.wait_ge(moved[j], 16 * TB * TOPK * b)
                sp.dma_start(rows[:, j, 0], batch_rows(xn_rows, 2 * b + j)).then_inc(rows_in[j], 16)

            sp.wait_ge(norms_ready, NB)
            load_rows(0, 0)
            load_rows(0, 1)
            load_xt(1)
            for q in range(3):
                spread_k(q, q)
            sp.wait_ge(zeroed, 16)
            sp.wait_ge(lasts_ready, 1)
            for e in range(E):
                k = sp.value_load(last_i[0:1, e:e + 1], min_val=0, max_val=FFN_TILES + E - 1)
                nothing = zeros[:].rearrange("p (a d) -> p a d", a=1).broadcast_to([P, FJ, D])
                sp.dma_start(tile_rows(slot_x, k), nothing).then_inc(padded, 16)

            def load_acc(first, tiles):
                acc_rows = x.rearrange("b (t p) d -> p (b t) d", p=P)
                sp.dma_start(acc[:, first:first + tiles, :], acc_rows[:, first:first + tiles, :]).then_inc(acc_in, 16)
            load_acc(0, T // 2)

            def body(b, second=False, last=False):
                n = NQ * b
                spread_k(n + 3, 3)
                if second and not known(b, HALF):
                    count = counted_by(sp, 2 * TB * TOPK * (b - HALF))
                    sp.wait_ge(made, 1)
                    sp.wait_ge(combined, count)
                    sp.wait_ge(added, b - 1)
                    k = 2 * (b - HALF - 1)
                    sp.dma_start(batch_rows(out, k), acc[:, at(TB * k, TB), :]).then_inc(stored, 16)
                    sp.dma_start(batch_rows(out, k + 1), acc[:, at(TB * (k + 1), TB), :]).then_inc(stored, 16)
                if not (last or known(b, HALF - 1)):
                    spread_k(n + NQ, 0)
                    if not known(b, NB - 2):
                        load_xt(b + 2)
                    spread_k(n + NQ + 1, 1)
                    if not second:
                        load_rows(b + 1, 0)
                    spread_k(n + NQ + 2, 2)
                    if not second:
                        load_rows(b + 1, 1)

            def load_tile(k, s):
                if some(k - 1):
                    sp.wait_ge(xgtr_done, k - 1)
                sp.dma_start(xg[:, s], tile_rows(slot_x, k)).then_inc(xg_in[s], 16)

            def store_tile(k, s):
                sp.wait_ge(ys_ready, k + 1)
                sp.dma_start(tile_rows(slot_y, k), ys[:, s]).then_inc(y_out[s], 16)

            def between():
                for j in range(2):
                    sp.wait_ge(moved[j], 16 * TB * TOPK * HALF)
                for k in range(3):
                    load_tile(k, k % 2)

                def step(k, s):
                    if not isinstance(k, int) or k + 3 < FFN_TILES:
                        load_tile(k + 3, 1 - s)
                    if not known(k, 0):
                        store_tile(k - 1, 1 - s)
                    if isinstance(k, int) and k < 3:
                        spread_k(NQ * HALF + k, k)
                    if known(k, 3):
                        load_xt(HALF + 1)
                    if isinstance(k, int) and k < 4:
                        load_acc(T // 2 + T // 8 * k, T // 8)
                expert_tiles(sp, step)
                store_tile(FFN_TILES - 1, (FFN_TILES - 1) % 2)

            attention(sp, body, between)
            sp.wait_ge(combined, 2 * TB * TOPK * (NB - HALF))
            sp.wait_ge(added, NB)
            for k in (NB - 2, NB - 1):
                sp.dma_start(batch_rows(out, k), acc[:, at(TB * k, TB), :]).then_inc(stored, 16)
            sp.wait_ge(stored, 16 * NB)

        @block.gpsimd
        def _(pool):
            pool.memset(zeros[:], 0.0).then_inc(zero_made, 1)
            pool.memset(identf[:], 1.0)
            pool.memset(identh[:], 1.0)
            pool.memset(before[:], 1.0)
            pool.memset(causal[:], 1.0)
            pool.iota(consti[:, 0:E], pattern=[[-1, E]], base=E, channel_multiplier=0)
            pool.iota(consti[:, E:], pattern=[[FT, FFN_TILES]], base=0, channel_multiplier=0)
            pool.memset(ones[:], 1.0).then_inc(made, 1)
            pool.wait_ge(made, 1)
            for m in (identf, identh):
                pool.affine_select(out=m[:], in_=m[:], compare_op=ALU.is_equal, fill=0.0, base=0,
                                   pattern=[[-1, P]], channel_multiplier=1)
            pool.affine_select(out=before[:], in_=before[:], compare_op=ALU.is_gt, fill=0.0, base=0,
                               pattern=[[1, P]], channel_multiplier=-1)
            pool.affine_select(out=causal[:], in_=causal[:], compare_op=ALU.is_ge, fill=0.0, base=0,
                               pattern=[[1, P]], channel_multiplier=-1).then_inc(made, 1)
            pool.tensor_copy(back[:], consti[:, 0:E])
            pool.tensor_copy(starts[:], consti[:, E:])
            pool.memset(v[:], 1.0)
            pool.memset(cnt[:], 0.0).then_inc(made, 1)
            pool.memset(ks[:], 0.0).then_inc(made, 1)
            pool.wait_ge(residue_ready, 2)
            for c in range(T * E // P):
                same = residue[:].rearrange("p (a e) -> p a e", a=1).broadcast_to([P, T, E])
                ins = pool.affine_select(out=later[:, c], in_=same, compare_op=ALU.is_gt, fill=0.0, base=-P * c,
                                         pattern=[[E, T], [1, E]], channel_multiplier=-1)
            ins.then_inc(later_ready, 1)

            def sum_squares(i):
                for s in range(2):
                    b = 2 * i + s
                    src = sq[:, s].rearrange("p t (h d) -> p t h d", d=DH)
                    count = counted_by(pool, TB * (b + 1))
                    pool.wait_ge(made, 1)
                    pool.wait_ge(sq_ready, count)
                    if some(b):
                        count = counted_by(pool, b)
                        pool.wait_ge(ss_ready, count)
                    pool.tensor_tensor(half_sums, src[:, :, :, 0:4], src[:, :, :, 4:8], ALU.add).then_inc(halves, 1)
                    pool.wait_ge(halves, 2 * b + 1)
                    pool.tensor_tensor(quarter_sums, half_sums[:, :, :, 0:2], half_sums[:, :, :, 2:4], ALU.add)\
                        .then_inc(halves, 1)
                    pool.wait_ge(halves, 2 * b + 2)
                    if some(b - 1):
                        pool.wait_ge(norms_ready, b - 1)
                    pool.tensor_tensor(sums[:, s], quarter_sums[:, :, :, 0], quarter_sums[:, :, :, 1], ALU.add)\
                        .then_inc(ss_ready, 1)

            def step(i, par, j):
                if not known(i, 0):
                    sum_squares(i - 1)
            stage_a(pool, step)
            sum_squares(NB // 2 - 1)

            def move(b, j, t, second):
                if t == 0:
                    if some(16 * TB * TOPK * b):
                        pool.wait_ge(moved[j], 16 * TB * TOPK * b)
                    k = 2 * (b - HALF) + j if second else 2 * b + j
                    pool.tensor_copy(idx[:, j], slots[:, at(TB * k, TB), :]).then_inc(idx_ready, 1)
                    count = counted_by(pool, 2 * b + j + 1)
                    pool.wait_ge(made, 1)
                    pool.wait_ge(idx_ready, count)
                    if second:
                        count = counted_by(pool, 2 * TB * TOPK * (b - HALF) + (j - 1) * TB * TOPK)
                        pool.wait_ge(made, 1)
                        if some(count):
                            pool.wait_ge(combined, count)
                    else:
                        count = counted_by(pool, 16 * (b + 1))
                        pool.wait_ge(made, 1)
                        pool.wait_ge(rows_in[j], count)
                for c in range(TOPK):
                    where = bass.IndirectOffsetOnAxis(ap=idx[:, j, t, c:c + 1], axis=0)
                    if second:
                        pool.indirect_dma_start(rows[:, j, c, t, :], None, slot_y, where).then_inc(moved[j], 16)
                    else:
                        pool.indirect_dma_start(slot_x, where, rows[:, j, 0, t, :], None).then_inc(moved[j], 16)

            def body(b, second=False, last=False):
                if known(b, HALF):
                    for s in range(2):
                        pool.wait_ge(y_out[s], 16 * ((FFN_TILES + 1 - s) // 2))
                for q in range(NQ):
                    n = NQ * b + q
                    for g in range(1, QH, 2):
                        count = counted_by(pool, UN * n + g + 1)
                        pool.wait_ge(made, 1)
                        pool.wait_ge(exp_done, count)
                        p = prob[:, q % 2, g - 1:g + 1, DIAG:DIAG + 3 * P].rearrange("p g (a c) -> p g a c", a=3)
                        pool.affine_select(out=p, in_=p, compare_op=ALU.is_ge, fill=0.0, base=0,
                                           pattern=[[0, 2], [0, 3], [1, P]], channel_multiplier=-1).then_inc(masked, 1)
                        slot = 2 * q + g // 2
                        if known(b, 0) and slot == 3:
                            pool.wait_ge(routed, 1)
                            pool.wait_ge(padded, 16 * E)
                        order = [0], [1, 2], [3], [4], [5], [6, 7], [], []
                        if known(b, 0):
                            order = [], [], [], [0, 1], [2, 3], [4, 5], [6], [7]
                        for k in order[slot]:
                            move(b, k // TB, k % TB, second)
            attention(pool, body, lambda: None)

        @block.scalar
        def _(act):
            def deviation(i):
                for s in range(2):
                    act.wait_ge(mv_ready, 2 * i + s + 1)
                    act.activation(std[:, s], mv[:, s, :, 1], ACT.Sqrt).then_inc(std_ready, 1)

            def squares(i, s):
                for t in range(TB):
                    tile = TB * (2 * i + s) + t
                    if t == 0 and some(2 * i + s - 1):
                        act.wait_ge(ss_ready, 2 * i + s - 1)
                    act.wait_ge(joint_done, tile + 1)
                    act.activation(sq[:, s, t, :], psum[:, 2 + t, E:WV0], ACT.Square)
                    act.copy(logits[:, at(tile), :], psum[:, 2 + t, 0:E].rearrange("p (a e) -> p a e", a=1))\
                        .then_inc(sq_ready, 1)

            def roots(i):
                for s in range(2):
                    act.wait_ge(ss_ready, 2 * i + s + 1)
                    act.activation(norms[:, at(TB * (2 * i + s), TB), :], sums[:, s], ACT.Sqrt, scale=1.0 / UP ** 2)\
                        .then_inc(norms_ready, 1)

            def step(i, par, j):
                for s in range(2):
                    act.wait_ge(tr_done, 2 * i + s + 1)
                    if some(16 * j):
                        act.wait_ge(cols_out[par][s], 16 * j)
                        act.wait_ge(joint_done, TB * (2 * i + s - 3))
                    act.copy(xts[:, par, s], psum[:, s, :]).then_inc(xts_ready, 1)
                if not known(i, 0):
                    squares(i - 1, 0)
                if not known(i, NB // 2 - 1):
                    deviation(i + 1)
                if not known(i, 0):
                    squares(i - 1, 1)
                if not (known(i, 0) or known(i, 1)):
                    roots(i - 2)
                for k in range(2):
                    act.wait_ge(wtr_done, 2 * i + k + 1)
                    w = wexp[:, at(i), k * W2C:k * W2C + M]
                    act.copy(w, psum[:, 6 + k, :].rearrange("p (a m) -> p a m", a=1)).then_inc(wt_ready, 1)
            deviation(0)
            stage_a(act, step)
            for s in range(2):
                squares(NB // 2 - 1, s)
            roots(NB // 2 - 2)
            roots(NB // 2 - 1)

            for q in range(3):
                act.wait_ge(qktr_done, q + 1)
                act.copy(qks[:, q].rearrange("p a n -> p (a n)"), ps_pb).then_inc(qk_evac, 1)

            def copy_o(n):
                act.wait_ge(pv_done, n + 1)
                if some(n):
                    act.wait_ge(otr_done, n)
                act.copy(osb, ps_o).then_inc(o_evac, 1)

            def body(b, second=False, last=False):
                for q in range(NQ):
                    n = NQ * b + q
                    for u in range(UN):
                        act.wait_ge(scored, UN * n + u + 1)
                        if u == 0:
                            if some(n - 1):
                                act.wait_ge(pv_done, n - 1)
                        act.activation(prob[:, q % 2, u, :], score[(q + u) % 2], ACT.Exp,
                                       scale=SCALE / UP ** 2).then_inc(exp_done, 1)
                        if u == 3 and not (known(b, 0) and q == 0):
                            copy_o(n - 1)

            def gelus(k, s):
                for c in range(MC):
                    if c % 2 == 0:
                        act.wait_ge(hid_done, 2 * k + c // 2 + 1)
                    if c == 0:
                        if some(k - 1):
                            act.wait_ge(y_done, k - 1)
                    act.activation(hs[:, s, c, :], psum[:, 2 * s + c // 2, (c % 2) * FT:(c % 2 + 1) * FT],
                                   ACT.Gelu, bias=ws[:, s, B1C + c:B1C + c + 1]).then_inc(gelu_done, 1)

            def between():
                act.wait_ge(selected, T // ST)
                act.activation(gapx[:, 0, :], gap[:], ACT.Exp).then_inc(gap_exp, 1)
                expert_tiles(act, gelus)
            attention(act, body, between)
            copy_o(NQ * NB - 1)

        @block.tensor
        def _(pe):
            pe.wait_ge(made, 2)

            def joint(i, par):
                for s in range(2):
                    pe.wait_ge(xts_ready, 2 * i + s + 1)
                    for t in range(TB):
                        tile = TB * (2 * i + s) + t
                        if some(tile - TB + 1):
                            pe.wait_ge(sq_ready, tile - TB + 1)
                        pe.matmul(psum[:, 2 + t, 0:WV0], xts[:, par, s, t * P:(t + 1) * P], wall[:, 0:WV0],
                                  start=True, stop=True).then_inc(joint_done, 1)

            def step(i, par, j):
                for s in range(2):
                    pe.wait_ge(xn_ready, 2 * i + s + 1)
                    if some(2 * i + s - 1):
                        pe.wait_ge(xts_ready, 2 * i + s - 1)
                    for t in range(TB):
                        mm = pe.transpose(psum[:, s, t * P:(t + 1) * P], xns[:, s, t, :], identf[:])
                    mm.then_inc(tr_done, 1)
                if known(i, 1):
                    pe.wait_ge(w_in, 48)
                if not known(i, 0):
                    joint(i - 1, 1 - par)
                pe.wait_ge(wn_in, 32 * (i + 1))
                if some(2 * i):
                    pe.wait_ge(wt_ready, 2 * i)
                for c in range(MC):
                    mm = pe.transpose(psum[:, 6, c * P:(c + 1) * P], w1n[:, c, :], identf[:])
                mm.then_inc(wtr_done, 1)
                for c in range(MC):
                    mm = pe.transpose(psum[:, 7, c * P:(c + 1) * P], w2n[:, c * P:(c + 1) * P], identf[:])
                mm.then_inc(wtr_done, 1)
            stage_a(pe, step)
            def project(b, t):
                tile = TB * b + t
                if t == 0:
                    pe.wait_ge(xt_in, 16 * (b + 1))
                    if some(b - 2):
                        pe.wait_ge(added, b - 2)
                if not known(b, 0):
                    pe.wait_ge(proj_evac, tile)
                bank = psum[:, t, :] if known(b, 0) else ps_pa
                pe.matmul(bank[:, 0:3 * D], xt[:, t * P:(t + 1) * P], wall[:, E:WEND],
                          start=True, stop=True).then_inc(proj_done, 1)

            def turn_qk(b, q):
                m = NQ * b + q
                pe.wait_ge(dup_done, TB * (b + 1))
                if some(m):
                    pe.wait_ge(qk_evac, m)
                for side in range(2):
                    for t in range(TB):
                        src = dup[:, t, side, QH * q:QH * (q + 1), :].rearrange("p h c -> p (h c)")
                        mm = pe.transpose(ps_pb[:, side * N + t * P:side * N + (t + 1) * P], src, identh[:])
                mm.then_inc(qktr_done, 1)

            def scores(b, q, u):
                n = NQ * b + q
                if u == 0:
                    pe.wait_ge(qk_evac, n + 1)
                    pe.wait_ge(ks_in[q], 16 * QH * (b + 1))
                if some(UN * n + u - 1):
                    pe.wait_ge(exp_done, UN * n + u - 1)
                s = score[(q + u) % 2]
                if u < QH:
                    parts = [(u, *part) for part in PARTS]
                else:
                    parts = [(g, 2, g * 2 * P, 2 * P, 2 * P) for g in range(QH)]
                for g, kt, col, first, cols in parts:
                    mm = pe.matmul(s[:, col:col + cols], ks[:, g, q, kt * P:(kt + 1) * P],
                                   qks[:, q, 0, first:first + cols], start=True, stop=True)
                mm.then_inc(scored, 1)

            def weigh(n, q, parts):
                for i in parts:
                    kt, col, first, cols = PARTS[i] if i < 4 else (2, None, 2 * P, 2 * P)
                    if i == 0:
                        if some(n):
                            pe.wait_ge(o_evac, n)
                        pe.wait_ge(exp_done, UN * n + QH)
                    if i == 1:
                        pe.wait_ge(masked, QH // 2 * (n + 1))
                    if i == 4:
                        pe.wait_ge(masked2, n + 1)
                    for g in range(QH):
                        u, c = (g, col) if i < 4 else (QH, g * 2 * P)
                        h = QH * q + g
                        mm = pe.matmul(ps_o[32 * g:32 * g + DH + 1, first:first + cols], v[:, kt * H + h, :],
                                       prob[:, q % 2, u, c:c + cols], start=(i == 0), stop=(i == 4),
                                       skip_group_check=True)
                if parts[-1] == 4:
                    mm.then_inc(pv_done, 1)

            def turn_o(n):
                pe.wait_ge(o_evac, n + 1)
                for t in range(TB):
                    mm = pe.transpose(ps_pc[:, t * P:(t + 1) * P], osb[:, t * P:(t + 1) * P], identf[:])
                mm.then_inc(otr_done, 1)

            def turn_on(b):
                pe.wait_ge(norm_done, NQ * (b + 1))
                for t in range(TB):
                    mm = pe.transpose(ps_pc[:, t * P:(t + 1) * P], on[:, t, :], identf[:])
                mm.then_inc(ontr_done, 1)

            def out_project(b, projected):
                pe.wait_ge(ot_ready, b + 1)
                pe.wait_ge(proj_evac, projected)
                for t in range(TB):
                    mm = pe.matmul(ps_pa[:, t * D:(t + 1) * D], ot[:, t * P:(t + 1) * P], wo[:],
                                   start=True, stop=True)
                mm.then_inc(outp_done, 1)

            pe.wait_ge(wv_in, 32)
            pe.wait_ge(xts_ready, NB)
            project(0, 0)
            project(0, 1)
            joint(NB // 2 - 1, 1)
            pe.wait_ge(sq_ready, T)
            project(0, 2)
            project(0, 3)
            pe.wait_ge(b1_in, 16)
            pe.wait_ge(wt_ready, 2 * (NB // 2))
            pe.transpose(psum[:, 6, 0:E * MC], b1n[:], identf[0:E * MC, 0:E * MC]).then_inc(btr_done, 1)
            pe.wait_ge(selected, T // ST)
            flat_both = both[:].rearrange("p t e -> p (t e)")
            for c in range(T * E // P):
                mm = pe.matmul(ps_o[:, c * P:(c + 1) * P], flat_both[:, c * P:(c + 1) * P], ones[:],
                               start=True, stop=True)
            mm.then_inc(counted, 1)
            pe.wait_ge(totals_read, 1)
            pe.wait_ge(later_ready, 1)
            for c in range(T * E // P):
                mm = pe.matmul(ps_o[:, 0:E], totals[:, c, :], residue[:], start=(c == 0), stop=(c == T * E // P - 1))
            mm.then_inc(counted, 1)
            pe.matmul(ps_pc, before[:], flat_both, start=True, stop=False)
            for c in range(T * E // P):
                mm = pe.matmul(ps_pc, totals[:, c, :], later[:, c].rearrange("p t e -> p (t e)"),
                               start=False, stop=(c == T * E // P - 1))
            mm.then_inc(placed, 1)
            pe.wait_ge(bt_ready, 1)
            for q in range(3):
                turn_qk(0, q)
            pe.wait_ge(v_ready, 1)

            def body(b, second=False, last=False):
                if known(b, HALF):
                    pe.wait_ge(gelu_done, MC * FFN_TILES)
                    pe.wait_ge(ys_ready, FFN_TILES)
                for q in range(NQ):
                    n = NQ * b + q
                    scores(b, q, 0)
                    if not (known(b, 0) and q < 2):
                        if q == 2:
                            if some(b):
                                pe.wait_ge(ot_ready, b)
                        if some(n - 2):
                            pe.wait_ge(norm_done, n - 2)
                        turn_o(n - 2)
                    if q == 2 and not last:
                        project(b + 1, 3)
                    scores(b, q, 1)
                    before_this = not (known(b, 0) and q == 0)
                    if before_this:
                        if q == 1:
                            pe.wait_ge(v_ready, b + 1)
                            if known(b, 0):
                                pe.wait_ge(routed, 1)
                        weigh(n - 1, (q - 1) % NQ, [0])
                    scores(b, q, 2)
                    if before_this:
                        weigh(n - 1, (q - 1) % NQ, [1, 3])
                    if q == 0:
                        turn_qk(b, 3)
                    elif not last:
                        if q == 1:
                            project(b + 1, 1)
                        elif q == 3:
                            turn_qk(b + 1, 1)
                    if q == 3 and not known(b, 0):
                        out_project(b - 1, TB * (b + 1) if last else TB * (b + 2))
                    scores(b, q, 3)
                    if before_this:
                        weigh(n - 1, (q - 1) % NQ, [2, 4])
                    if q == 1 and not known(b, 0):
                        turn_on(b - 1)
                    scores(b, q, 4)
                    if not last:
                        if q == 0:
                            project(b + 1, 0)
                        elif q == 1:
                            project(b + 1, 2)
                        elif q == 2:
                            turn_qk(b + 1, 0)
                        else:
                            turn_qk(b + 1, 2)

            def between():
                pe.wait_ge(exp_done, UN * NQ * HALF)
                pe.wait_ge(o_evac, NQ * HALF - 1)
                pe.wait_ge(proj_evac, TB * (HALF + 1))
                pe.wait_ge(qk_evac, NQ * HALF + 3)
                pe.wait_ge(norm_done, NQ * HALF - 2)
                pe.wait_ge(added, HALF - 1)

                def turn_x(k, s):
                    pe.wait_ge(xg_in[s], 8 * (k - s) + 16)
                    if some(k - 1):
                        pe.wait_ge(xgt_ready, k - 1)
                    for j in range(FJ):
                        mm = pe.transpose(psum[:, 4 + s, j * P:(j + 1) * P], xg[:, s, j, :], identf[:])
                    mm.then_inc(xgtr_done, 1)

                def hidden(k, s):
                    pe.wait_ge(xgt_ready, k + 1)
                    pe.wait_ge(w1_ready, k + 1)
                    if some(MC * (k - 1)):
                        pe.wait_ge(gelu_done, MC * (k - 1))
                    for c in range(MC):
                        mm = pe.matmul(psum[:, 2 * s + c // 2, (c % 2) * FT:(c % 2 + 1) * FT],
                                       ws[:, s, c * P:(c + 1) * P], xgt[:, s, :], start=True, stop=True)
                        if c % 2:
                            mm.then_inc(hid_done, 1)

                def outputs(k, s):
                    pe.wait_ge(w2_ready, k + 1)
                    pe.wait_ge(gelu_done, MC * (k + 1))
                    if some(k - 1):
                        pe.wait_ge(ys_ready, k - 1)
                    for j in range(FJ):
                        for c in range(MC):
                            mm = pe.matmul(psum[:, 6 + s, j * D:(j + 1) * D], hs[:, s, c, j * P:(j + 1) * P],
                                           ws[:, s, W2C + c * D:W2C + (c + 1) * D],
                                           start=(c == 0), stop=(c == MC - 1))
                    mm.then_inc(y_done, 1)

                turn_x(0, 0)

                def step(k, s):
                    if not isinstance(k, int) or k + 1 < FFN_TILES:
                        turn_x(k + 1, 1 - s)
                    hidden(k, s)
                    if not known(k, 0):
                        outputs(k - 1, 1 - s)
                expert_tiles(pe, step)
                outputs(FFN_TILES - 1, (FFN_TILES - 1) % 2)

            attention(pe, body, between)
            n = NQ * NB
            pe.wait_ge(norm_done, n - 2)
            turn_o(n - 2)
            weigh(n - 1, NQ - 1, [0, 1, 3, 2, 4])
            pe.wait_ge(norm_done, n - 1)
            turn_o(n - 1)
            turn_on(NB - 1)
            pe.wait_ge(added, NB - 1)
            out_project(NB - 1, TB * NB)

        @block.vector
        def _(dve):
            back_t = back[:].rearrange("p (a e) -> p a e", a=1).broadcast_to([P, ST, E])

            def by_expert(ap):
                return ap.rearrange("p (t a) -> p t a", a=1).broadcast_to([P, ST, E])

            def select(h, c):
                tiles = at(ST * h, ST)
                src = spent[:] if c else logits[:, tiles, :]
                k = SELECT * h + 6 * c
                if c == 0:
                    count = counted_by(dve, ST * (h + 1))
                    dve.wait_ge(made, 1)
                    dve.wait_ge(sq_ready, count)
                    if some(h):
                        dve.wait_ge(selected, h)
                else:
                    dve.wait_ge(sel, k)
                dve.tensor_reduce(top[:, c], src, AX.X, ALU.max).then_inc(sel, 1)
                dve.wait_ge(sel, k + 1)
                dve.tensor_tensor(mark[:], src, by_expert(top[:, c]), ALU.is_equal).then_inc(sel, 1)
                dve.wait_ge(sel, k + 2)
                dve.tensor_tensor(mark[:], mark[:], back_t, ALU.mult).then_inc(sel, 1)
                dve.wait_ge(sel, k + 3)
                dve.tensor_reduce(rank[:, c], mark[:], AX.X, ALU.max).then_inc(sel, 1)
                dve.wait_ge(sel, k + 4)
                dve.tensor_tensor(hot[:, c, tiles, :], mark[:], by_expert(rank[:, c]), ALU.is_equal).then_inc(sel, 1)
                dve.wait_ge(sel, k + 5)
                if c == 0:
                    dve.scalar_tensor_tensor(out=spent[:], in0=hot[:, 0, tiles, :], scalar=-3.0e38, in1=src,
                                             op0=ALU.mult, op1=ALU.add).then_inc(sel, 1)
                else:
                    dve.tensor_tensor(both[:, tiles, :], hot[:, 0, tiles, :], hot[:, 1, tiles, :], ALU.add)
                    dve.tensor_tensor(gap[:, tiles], top[:, 1], top[:, 0], ALU.subtract).then_inc(selected, 1)

            def statistics(i, par, j):
                for s in range(2):
                    dve.wait_ge(xs_in[par][s], 16 * (j + 1))
                    if some(2 * i + s - 1):
                        dve.wait_ge(mv_ready, 2 * i + s - 1)
                    for t in range(TB):
                        ins = dve.bn_stats(bst[:, s, t, :], xs[:, par, s, t, :])
                    ins.then_inc(stats, 1)
                for s in range(2):
                    count = counted_by(dve, 2 * i + s + 1)
                    dve.wait_ge(made, 1)
                    dve.wait_ge(stats, count)
                    if some(2 * i + s - 1):
                        dve.wait_ge(xn_ready, 2 * i + s - 1)
                    for t in range(TB):
                        ins = dve.bn_aggr(mv[:, s, t, :], bst[:, s, t, :])
                    ins.then_inc(r_step, 1)
                for s in range(2):
                    dve.wait_ge(r_step, 2 * i + 2)
                    if some(2 * i + s - 1):
                        dve.wait_ge(std_ready, 2 * i + s - 1)
                    dve.tensor_scalar(mv[:, s, :, 1], mv[:, s, :, 1], LN_EPS, None, ALU.add).then_inc(mv_ready, 1)

            def normalise(i, par):
                for s in range(2):
                    dve.wait_ge(std_ready, 2 * i + s + 1)
                    if some(2 * i + s - 1):
                        dve.wait_ge(xn_ready, 2 * i + s - 1)
                    dve.reciprocal(rstd[:, s], std[:, s]).then_inc(rstd_ready, 1)
                    dve.wait_ge(rstd_ready, 2 * i + s + 1)
                    if some(2 * i + s - 1):
                        dve.wait_ge(tr_done, 2 * i + s - 1)
                    if some(16 * i):
                        dve.wait_ge(rows_out[s], 16 * i)
                    for t in range(TB):
                        ins = dve.tensor_scalar(xns[:, s, t, :], xs[:, par, s, t, :], mv[:, s, t, 0:1],
                                                rstd[:, s, t:t + 1], ALU.subtract, ALU.mult)
                    ins.then_inc(xn_ready, 1)

            def step(i, par, j):
                normalise(i, par)
                if not known(i, NB // 2 - 1):
                    statistics(i + 1, 1 - par, j + par)
                if known(i, 3):
                    dve.wait_ge(made, 3)
                if par == 1 and not known(i, 1):
                    select(j - 1, 0)
                if par == 0 and not (known(i, 0) or known(i, 2)):
                    select(j - 2, 1)
            statistics(0, 0, 0)
            dve.wait_ge(made, 2)
            dve.tensor_reduce(mark[:, 0, :], identf[:].rearrange("p (j e) -> p e j", e=E), AX.X, ALU.add)\
                .then_inc(residue_ready, 1)
            dve.wait_ge(residue_ready, 1)
            dve.tensor_copy(residue[:], mark[:, 0, :]).then_inc(residue_ready, 1)
            stage_a(dve, step)
            steps = NB

            def next_step():
                nonlocal steps
                steps += 1
                return steps

            def prepare(b, t):
                tile = TB * b + t
                if t == 0:
                    if some(tile):
                        dve.wait_ge(qn_done, tile)
                    dve.tensor_scalar(rnb[:], norms[:, at(TB * b, TB), :], NORM_EPS / UP, None, ALU.max)\
                        .then_inc(rn_done, 1)
                    dve.wait_ge(rn_done, 2 * b + 1)
                    dve.reciprocal(rnb[:], rnb[:]).then_inc(rn_done, 1)
                    dve.wait_ge(rn_done, 2 * b + 2)
                    if some(NQ * b):
                        dve.wait_ge(qktr_done, NQ * b)
                    if some(b):
                        dve.wait_ge(v_ready, b)
                dve.wait_ge(proj_done, tile + 1)
                if some(tile):
                    dve.wait_ge(dup_done, tile)
                bank = psum[:, t, :] if known(b, 0) else ps_pa
                scale = rnb[:, t, :].rearrange("p (h a) -> p h a", a=1).broadcast_to([P, NQK, DH])
                dve.tensor_tensor(qn[:], bank[:, 0:2 * D].rearrange("p (h d) -> p h d", d=DH), scale, ALU.mult)\
                    .then_inc(qn_done, 1)
                dve.tensor_copy(vn[:, t * H:(t + 1) * H, :], bank[:, 2 * D:3 * D].rearrange("p (h d) -> p h d", d=DH))\
                    .then_inc(proj_evac, 1)
                dve.wait_ge(qn_done, tile + 1)
                q_to = dup[:, t, 0].rearrange("p h (a b d) -> p h a b d", a=2, b=2)
                k_to = dup[:, t, 1].rearrange("p h (a b d) -> p h a b d", a=2, b=2)

                def twice(ap):
                    return ap.rearrange("p h (a d) -> p h a d", a=1).broadcast_to([P, H, 2, DH])
                q32, k32 = twice(qn[:, 0:H, :]), twice(qn[:, H:NQK, :])
                dve.tensor_copy(q_to[:, :, :, 0, :], q32)
                dve.tensor_copy(k_to[:, :, 0, :, :], k32).then_inc(hi_done, 1)
                dve.wait_ge(hi_done, tile + 1)
                dve.tensor_tensor(q_to[:, :, :, 1, :], q32, q_to[:, :, :, 0, :], ALU.subtract)
                dve.tensor_tensor(k_to[:, :, 1, :, :], k32, k_to[:, :, 0, :, :], ALU.subtract).then_inc(dup_done, 1)

            def copy_qk(b, q):
                m = NQ * b + q
                dve.wait_ge(qktr_done, m + 1)
                if some(UN * (m - NQ + 1)):
                    dve.wait_ge(scored, UN * (m - NQ + 1))
                dve.tensor_copy(qks[:, q].rearrange("p a n -> p (a n)"), ps_pb).then_inc(qk_evac, 1)

            def copy_v(b):
                dve.wait_ge(proj_evac, TB * (b + 1))
                if some(NQ * b):
                    dve.wait_ge(pv_done, NQ * b)
                dve.tensor_copy(v[:, :, 0:DH], vn[:]).then_inc(v_ready, 1)

            select(T // ST - 2, 1)
            dve.wait_ge(norms_ready, 1)
            prepare(0, 0)
            prepare(0, 1)
            for c in range(TOPK):
                select(T // ST - 1, c)
            dve.wait_ge(btr_done, 1)
            dve.tensor_copy(wexp[:, :, B1C:W2C], psum[:, 6, 0:E * MC].rearrange("p (e c) -> p e c", e=E))\
                .then_inc(bt_ready, 1)
            dve.wait_ge(counted, 1)
            dve.tensor_copy(totals.rearrange("p c n -> p (c n)"), ps_o).then_inc(totals_read, 1)
            for t in range(2, TB):
                prepare(0, t)
            copy_v(0)
            dve.wait_ge(counted, 2)
            rows_of = cnt[:, 0, 0:E]
            dve.tensor_copy(rows_of, ps_o[:, 0:E]).then_inc(r_step, 1)
            dve.wait_ge(r_step, next_step())
            dve.tensor_scalar(cnti[:, 0], rows_of, float(FT - 1), None, ALU.add).then_inc(r_step, 1)
            dve.wait_ge(r_step, next_step())
            dve.tensor_scalar(cnti[:, 1], cnti[:, 0], FSH, FSH, ALU.logical_shift_right, ALU.logical_shift_left)\
                .then_inc(r_step, 1)
            dve.wait_ge(r_step, next_step())
            dve.tensor_copy(cnt[:, 1, E:], cnti[:, 1]).then_inc(r_step, 1)
            dve.wait_ge(r_step, next_step())
            level, shift = 1, 1
            while shift < E:
                dve.tensor_tensor(cnt[:, level + 1, E:], cnt[:, level, E:], cnt[:, level, E - shift:2 * E - shift],
                                  ALU.add).then_inc(r_step, 1)
                dve.wait_ge(r_step, next_step())
                level, shift = level + 1, 2 * shift
            ends = cnt[:, level, E:]
            dve.tensor_tensor(cnt[:, 0, E:], ends, cnt[:, 1, E:], ALU.subtract).then_inc(r_step, 1)
            dve.wait_ge(r_step, next_step())
            dve.tensor_scalar(lastf[:, 0], ends, 1.0 / FT, -1.0, ALU.mult, ALU.add).then_inc(r_step, 1)
            dve.tensor_scalar(lastf[:, 1], rows_of, 0.0, None, ALU.is_gt).then_inc(r_step, 1)
            dve.wait_ge(r_step, next_step())
            dve.tensor_tensor(lastf[:, 2], lastf[:, 0], back[:], ALU.add).then_inc(r_step, 1)
            next_step()
            dve.wait_ge(r_step, next_step())
            dve.scalar_tensor_tensor(out=lastf[:, 3], in0=lastf[:, 2], scalar=-float(FFN_TILES + E), in1=lastf[:, 1],
                                     op0=ALU.add, op1=ALU.mult).then_inc(r_step, 1)
            dve.wait_ge(r_step, next_step())
            dve.scalar_tensor_tensor(out=last_i[:], in0=lastf[:, 3], scalar=float(FFN_TILES + E), in1=back[:],
                                     op0=ALU.add, op1=ALU.subtract).then_inc(lasts_ready, 1)
            dve.wait_ge(placed, 1)
            dve.wait_ge(norms_ready, NB)
            base = cnt[:, 0:1, E:].broadcast_to([P, T, E])
            dve.tensor_tensor(place, ps_pc.rearrange("p (t e) -> p t e", e=E), base, ALU.add).then_inc(r_step, 1)
            dve.wait_ge(r_step, next_step())
            for c in range(TOPK):
                dve.tensor_tensor(mine, hot[:, c], place, ALU.mult).then_inc(r_step, 1)
                dve.wait_ge(r_step, next_step())
                with nc.allow_low_precision(reason="one number that isn't zero, and whole"):
                    dve.tensor_reduce(slots[:, :, c], mine, AX.X, ALU.add).then_inc(r_step, 1)
                dve.wait_ge(r_step, next_step())
            dve.memset(ps_o, 0.0).then_inc(r_step, 1)
            dve.wait_ge(r_step, next_step())
            dve.sem_inc(routed, 1)
            dve.tensor_scalar(tile_f[:, 0], starts[:], ends[:, 0:1], None, ALU.is_ge).then_inc(r_step, 1)
            dve.wait_ge(r_step, next_step())
            for e in range(1, E - 1):
                dve.scalar_tensor_tensor(out=tile_f[:, e % 2], in0=starts[:], scalar=ends[:, e:e + 1],
                                         in1=tile_f[:, (e - 1) % 2], op0=ALU.is_ge, op1=ALU.add).then_inc(r_step, 1)
                dve.wait_ge(r_step, next_step())
            dve.tensor_copy(tile_i[:], tile_f[:, (E - 2) % 2]).then_inc(r_step, 1)
            dve.wait_ge(r_step, next_step())

            def mask2(n, q):
                dve.wait_ge(exp_done, UN * (n + 1))
                p = prob[:, q % 2, QH, :].rearrange("p (g c) -> p g c", g=QH)[:, :, 0:P]
                dve.tensor_tensor(p, p, causal[:].rearrange("p (a c) -> p a c", a=1).broadcast_to([P, QH, P]), ALU.mult)\
                    .then_inc(masked2, 1)

            def divide(n, q):
                dve.wait_ge(otr_done, n + 1)
                o = ps_pc.rearrange("p (t g c) -> p t g c", t=TB, g=QH)
                if some(n):
                    dve.wait_ge(norm_done, n)
                dve.reciprocal(rs[:], o[:, :, :, DH]).then_inc(rs_done, 1)
                dve.wait_ge(rs_done, n + 1)
                to = on.rearrange("p t (q g d) -> p t q g d", q=NQ, g=QH)[:, :, q]
                dve.tensor_tensor(to, o[:, :, :, 0:DH],
                                  rs[:].rearrange("p t (g a) -> p t g a", a=1).broadcast_to([P, TB, QH, DH]), ALU.mult)\
                    .then_inc(norm_done, 1)

            def add_attention(b, combines):
                dve.wait_ge(outp_done, b + 1)
                if some(combines):
                    dve.wait_ge(combined, combines)
                if known(b, 0):
                    dve.wait_ge(acc_in, 16)
                a = acc[:, at(TB * b, TB), :]
                dve.tensor_tensor(a, ps_pa.rearrange("p (t d) -> p t d", t=TB), a, ALU.add).then_inc(added, 1)

            def combine(b, j, adds):
                k = 2 * (b - HALF) + j
                dve.wait_ge(moved[j], 16 * TB * TOPK * (b + 1))
                dve.wait_ge(added, adds)
                for c in range(TOPK):
                    if some(TB * TOPK * k + TB * c):
                        dve.wait_ge(combined, TB * TOPK * k + TB * c)
                    for t in range(TB):
                        a = acc[:, at(TB * k + t), :]
                        r = rows[:, j, c, t:t + 1, :]
                        dve.scalar_tensor_tensor(out=a, in0=r, scalar=gate[:, c, at(TB * k + t)], in1=a,
                                                 op0=ALU.mult, op1=ALU.add).then_inc(combined, 1)

            def body(b, second=False, last=False):
                each = TB * TOPK
                for q in range(NQ):
                    n = NQ * b + q
                    if not (known(b, 0) and q == 0):
                        mask2(n - 1, (q - 1) % NQ)
                    if not (known(b, 0) and q < 2):
                        if q == 2:
                            if some(b):
                                dve.wait_ge(ontr_done, b)
                        divide(n - 2, (q - 2) % NQ)
                    if q == 0:
                        copy_qk(b, 3)
                    elif not last:
                        if q == 1:
                            prepare(b + 1, 1)
                        elif q == 2:
                            prepare(b + 1, 3)
                        else:
                            copy_qk(b + 1, 1)
                    if q == 3 and not known(b, 0):
                        add_attention(b - 1, each * (2 * (b - HALF) + 1) if second else 0)
                    if q == 0 and not known(b, 0):
                        copy_v(b)
                    if q == 1 and not known(b, 0):
                        dve.wait_ge(ontr_done, b)
                        if some(b - 1):
                            dve.wait_ge(outp_done, b - 1)
                        dve.tensor_copy(ot, ps_pc).then_inc(ot_ready, 1)
                    if not last:
                        if q == 0:
                            prepare(b + 1, 0)
                        elif q == 1:
                            prepare(b + 1, 2)
                        elif q == 2:
                            copy_qk(b + 1, 0)
                        else:
                            copy_qk(b + 1, 2)
                    if second and q >= 2 and not (last and q == 3):
                        combine(b, q - 2, b - 1 if q == 2 else b)

            def between():
                dve.wait_ge(gap_exp, 1)
                dve.tensor_scalar(gapx[:, 1], gapx[:, 0], 1.0, None, ALU.add).then_inc(r_step, 1)
                dve.wait_ge(r_step, next_step())
                dve.reciprocal(gate[:, 0], gapx[:, 1]).then_inc(r_step, 1)
                dve.wait_ge(r_step, next_step())
                dve.tensor_tensor(gate[:, 1], gate[:, 0], gapx[:, 0], ALU.mult).then_inc(r_step, 1)
                dve.wait_ge(r_step, next_step())
                dve.wait_ge(b2_in, 16)
                dve.wait_ge(bt_ready, 1)
                dve.wait_ge(wt_ready, 2 * (NB // 2))
                dve.wait_ge(pv_done, NQ * HALF - 1)

                def copy_w1(k, s):
                    e = dve.value_load(tile_i[0:1, at(k)], min_val=0, max_val=E - 1)
                    if some(k - 1):
                        dve.wait_ge(hid_done, 2 * (k - 1))
                        dve.wait_ge(gelu_done, MC * (k - 1))
                    dve.tensor_copy(ws[:, s:s + 1, 0:W2C], wexp[:, at(e), 0:W2C]).then_inc(w1_ready, 1)
                    return e

                def copy_w2(k, s, e):
                    if some(k - 1):
                        dve.wait_ge(y_done, k - 1)
                        dve.wait_ge(ys_ready, k - 1)
                    dve.tensor_copy(ws[:, s:s + 1, W2C:WX], wexp[:, at(e), W2C:WX]).then_inc(w2_ready, 1)

                def copy_x(k, s):
                    dve.wait_ge(xgtr_done, k + 1)
                    if some(2 * (k - 1)):
                        dve.wait_ge(hid_done, 2 * (k - 1))
                    dve.tensor_copy(xgt[:, s, :], psum[:, 4 + s, 0:FT]).then_inc(xgt_ready, 1)

                def copy_y(k, s):
                    dve.wait_ge(y_done, k + 1)
                    if some(8 * (k - s)):
                        dve.wait_ge(y_out[s], 8 * (k - s))
                    bias = ws[:, s:s + 1, B2C:WX].broadcast_to([P, FJ, D])
                    dve.tensor_tensor(ys[:, s], psum[:, 6 + s, 0:FT].rearrange("p (j d) -> p j d", j=FJ), bias, ALU.add)\
                        .then_inc(ys_ready, 1)

                e = copy_w1(0, 0)
                copy_w2(0, 0, e)
                copy_x(0, 0)

                def step(k, s):
                    more = not isinstance(k, int) or k + 1 < FFN_TILES
                    if more:
                        e = copy_w1(k + 1, 1 - s)
                        copy_x(k + 1, 1 - s)
                    if not known(k, 0):
                        copy_y(k - 1, 1 - s)
                    if more:
                        copy_w2(k + 1, 1 - s, e)
                expert_tiles(dve, step)
                copy_y(FFN_TILES - 1, (FFN_TILES - 1) % 2)
                dve.wait_ge(acc_in, 16 * 5)

            attention(dve, body, between)
            n = NQ * NB
            mask2(n - 1, NQ - 1)
            divide(n - 2, NQ - 2)
            combine(NB - 1, 1, NB - 1)
            divide(n - 1, NQ - 1)
            dve.wait_ge(ontr_done, NB)
            dve.wait_ge(outp_done, NB - 1)
            dve.tensor_copy(ot, ps_pc).then_inc(ot_ready, 1)
            add_attention(NB - 1, 2 * TB * TOPK * HALF)


_INS = ["L0_attn_x", "L0_attn_Wq", "L0_attn_Wk", "L0_attn_Wv", "L0_attn_Wo", "L0_ffn_Wr", "L0_ffn_W1", "L0_ffn_b1",
        "L0_ffn_W2", "L0_ffn_b2"]


def kernel(**inputs):
    import numpy as _np
    import concourse.bacc as _bacc
    from concourse.bass_utils import run_bass_kernel_spmd as _run

    nc = _bacc.Bacc("TRN2", target_bir_lowering=False, num_devices=1)
    arrays, args = {}, []
    for name in _INS:
        a = _np.ascontiguousarray(inputs[name])
        arrays[f"in_{name}"] = a
        args.append(nc.dram_tensor(f"in_{name}", a.shape, mybir.dt.from_np(a.dtype), kind="ExternalInput").ap())
    shape = arrays["in_L0_attn_x"].shape
    args.append(nc.dram_tensor("out_0", shape, F32, kind="ExternalOutput").ap())
    build(nc, *args)
    r = _run(nc, [arrays], core_ids=[0])
    return r.results[0]["out_0"]
```
